# Optimizing a Trainium2 kernel written in Bass

```python
import numpy as np
import jax
import jax.numpy as jnp

def _softmax(x, axis=-1):
    return jax.nn.softmax(x, axis=axis)

def _gelu(x):
    return jax.nn.gelu(x, approximate=True)

def _silu(x):
    return jax.nn.silu(x)

def _sigmoid(x):
    return jax.nn.sigmoid(x)

def _layernorm(x, axis=-1, eps=1e-05):
    m = jnp.mean(x, axis=axis, keepdims=True)
    v = jnp.var(x, axis=axis, keepdims=True)
    return (x - m) / jnp.sqrt(v + eps)

def _scatter_add(tgt, idx, src, axis=0):
    return tgt.at[idx].add(src)

def _segment_sum(src, seg, n):
    return jax.ops.segment_sum(src, seg, n)
kernel_name = 'mk_dlrm_tower_d1_rec_r8_bd780f'

def setup_inputs(seed: int=0):
    np.random.seed(seed)
    _w = jnp.asarray

    def _rec_inputs():
        import jax
        import jax.numpy as jnp
        _tk = jax.random.key(seed)
        ids = jnp.stack([jax.random.randint(jax.random.fold_in(_tk, 200 + f), (512,), 0, v, jnp.int32) for f, v in enumerate([12500, 1000, 1000, 12500, 1000, 12500, 1000, 1000, 1250, 125000, 1250, 12500, 1000, 1000, 1000, 12500, 12500, 1000, 1250, 1000, 1250, 1250, 1250, 1250, 1250, 12500, 12500, 1250, 1250, 1250, 1250, 1250, 1000])], axis=1)
        tbl_0 = 0.05 * jax.random.normal(jax.random.fold_in(_tk, 500 + 0), (12500, 128), jnp.float32)
        tbl_1 = 0.05 * jax.random.normal(jax.random.fold_in(_tk, 500 + 1), (1000, 128), jnp.float32)
        tbl_2 = 0.05 * jax.random.normal(jax.random.fold_in(_tk, 500 + 2), (1000, 128), jnp.float32)
        tbl_3 = 0.05 * jax.random.normal(jax.random.fold_in(_tk, 500 + 3), (12500, 128), jnp.float32)
        tbl_4 = 0.05 * jax.random.normal(jax.random.fold_in(_tk, 500 + 4), (1000, 128), jnp.float32)
        tbl_5 = 0.05 * jax.random.normal(jax.random.fold_in(_tk, 500 + 5), (12500, 128), jnp.float32)
        tbl_6 = 0.05 * jax.random.normal(jax.random.fold_in(_tk, 500 + 6), (1000, 128), jnp.float32)
        tbl_7 = 0.05 * jax.random.normal(jax.random.fold_in(_tk, 500 + 7), (1000, 128), jnp.float32)
        tbl_8 = 0.05 * jax.random.normal(jax.random.fold_in(_tk, 500 + 8), (1250, 128), jnp.float32)
        tbl_9 = 0.05 * jax.random.normal(jax.random.fold_in(_tk, 500 + 9), (125000, 128), jnp.float32)
        tbl_10 = 0.05 * jax.random.normal(jax.random.fold_in(_tk, 500 + 10), (1250, 128), jnp.float32)
        tbl_11 = 0.05 * jax.random.normal(jax.random.fold_in(_tk, 500 + 11), (12500, 128), jnp.float32)
        tbl_12 = 0.05 * jax.random.normal(jax.random.fold_in(_tk, 500 + 12), (1000, 128), jnp.float32)
        tbl_13 = 0.05 * jax.random.normal(jax.random.fold_in(_tk, 500 + 13), (1000, 128), jnp.float32)
        tbl_14 = 0.05 * jax.random.normal(jax.random.fold_in(_tk, 500 + 14), (1000, 128), jnp.float32)
        tbl_15 = 0.05 * jax.random.normal(jax.random.fold_in(_tk, 500 + 15), (12500, 128), jnp.float32)
        tbl_16 = 0.05 * jax.random.normal(jax.random.fold_in(_tk, 500 + 16), (12500, 128), jnp.float32)
        tbl_17 = 0.05 * jax.random.normal(jax.random.fold_in(_tk, 500 + 17), (1000, 128), jnp.float32)
        tbl_18 = 0.05 * jax.random.normal(jax.random.fold_in(_tk, 500 + 18), (1250, 128), jnp.float32)
        tbl_19 = 0.05 * jax.random.normal(jax.random.fold_in(_tk, 500 + 19), (1000, 128), jnp.float32)
        tbl_20 = 0.05 * jax.random.normal(jax.random.fold_in(_tk, 500 + 20), (1250, 128), jnp.float32)
        tbl_21 = 0.05 * jax.random.normal(jax.random.fold_in(_tk, 500 + 21), (1250, 128), jnp.float32)
        tbl_22 = 0.05 * jax.random.normal(jax.random.fold_in(_tk, 500 + 22), (1250, 128), jnp.float32)
        tbl_23 = 0.05 * jax.random.normal(jax.random.fold_in(_tk, 500 + 23), (1250, 128), jnp.float32)
        tbl_24 = 0.05 * jax.random.normal(jax.random.fold_in(_tk, 500 + 24), (1250, 128), jnp.float32)
        tbl_25 = 0.05 * jax.random.normal(jax.random.fold_in(_tk, 500 + 25), (12500, 128), jnp.float32)
        tbl_26 = 0.05 * jax.random.normal(jax.random.fold_in(_tk, 500 + 26), (12500, 128), jnp.float32)
        tbl_27 = 0.05 * jax.random.normal(jax.random.fold_in(_tk, 500 + 27), (1250, 128), jnp.float32)
        tbl_28 = 0.05 * jax.random.normal(jax.random.fold_in(_tk, 500 + 28), (1250, 128), jnp.float32)
        tbl_29 = 0.05 * jax.random.normal(jax.random.fold_in(_tk, 500 + 29), (1250, 128), jnp.float32)
        tbl_30 = 0.05 * jax.random.normal(jax.random.fold_in(_tk, 500 + 30), (1250, 128), jnp.float32)
        tbl_31 = 0.05 * jax.random.normal(jax.random.fold_in(_tk, 500 + 31), (1250, 128), jnp.float32)
        tbl_32 = 0.05 * jax.random.normal(jax.random.fold_in(_tk, 500 + 32), (1000, 128), jnp.float32)
        _rk = jax.random.fold_in(_tk, 7)
        r_gnn_feature = -0.00340659 + 1.00146 * jax.random.normal(jax.random.fold_in(_rk, 101), (512, 128), jnp.float32)
        W_top1 = 0.051031 * jax.random.normal(jax.random.fold_in(_tk, 801), (384, 512), jnp.float32)
        W_top2 = 0.0441942 * jax.random.normal(jax.random.fold_in(_tk, 802), (512, 256), jnp.float32)
        W_top3 = 0.0625 * jax.random.normal(jax.random.fold_in(_tk, 803), (256, 1), jnp.float32)
        b_top1 = jnp.zeros((512,), jnp.float32)
        b_top2 = jnp.zeros((256,), jnp.float32)
        return (r_gnn_feature, ids, tbl_0, tbl_1, tbl_2, tbl_3, tbl_4, tbl_5, tbl_6, tbl_7, tbl_8, tbl_9, tbl_10, tbl_11, tbl_12, tbl_13, tbl_14, tbl_15, tbl_16, tbl_17, tbl_18, tbl_19, tbl_20, tbl_21, tbl_22, tbl_23, tbl_24, tbl_25, tbl_26, tbl_27, tbl_28, tbl_29, tbl_30, tbl_31, tbl_32, W_top1, b_top1, W_top2, b_top2, W_top3)
    r_gnn_feature, ids, tbl_0, tbl_1, tbl_2, tbl_3, tbl_4, tbl_5, tbl_6, tbl_7, tbl_8, tbl_9, tbl_10, tbl_11, tbl_12, tbl_13, tbl_14, tbl_15, tbl_16, tbl_17, tbl_18, tbl_19, tbl_20, tbl_21, tbl_22, tbl_23, tbl_24, tbl_25, tbl_26, tbl_27, tbl_28, tbl_29, tbl_30, tbl_31, tbl_32, W_top1, b_top1, W_top2, b_top2, W_top3 = _rec_inputs()

    def _L0_rec_setup():
        import jax, jax.numpy as jnp
        import numpy as np
        B, F, D, A = (1024, 33, 128, 128)
        key = jax.random.key(seed)
        k1, k2, k3, k4 = jax.random.split(key, 4)
        gnn_feature = jax.random.normal(k1, (B, A), dtype=jnp.float32)
        x = jax.random.normal(k2, (B, F, D), dtype=jnp.float32)
        lim = 1.0 / np.sqrt(D)
        attn_W = jax.random.uniform(k3, (A, D), minval=-lim, maxval=lim, dtype=jnp.float32)
        attn_b = jax.random.uniform(k4, (A,), minval=-lim, maxval=lim, dtype=jnp.float32)
        return {'gnn_feature': gnn_feature, 'x': x, 'attn_W': attn_W, 'attn_b': attn_b}
    _L0_rec_all = _L0_rec_setup()
    _L0_rec_in = {k: v for k, v in _L0_rec_all.items() if k in ('attn_W', 'attn_b')}
    del _L0_rec_all
    return {'r_gnn_feature': r_gnn_feature, 'ids': ids, 'tbl_0': tbl_0, 'tbl_1': tbl_1, 'tbl_2': tbl_2, 'tbl_3': tbl_3, 'tbl_4': tbl_4, 'tbl_5': tbl_5, 'tbl_6': tbl_6, 'tbl_7': tbl_7, 'tbl_8': tbl_8, 'tbl_9': tbl_9, 'tbl_10': tbl_10, 'tbl_11': tbl_11, 'tbl_12': tbl_12, 'tbl_13': tbl_13, 'tbl_14': tbl_14, 'tbl_15': tbl_15, 'tbl_16': tbl_16, 'tbl_17': tbl_17, 'tbl_18': tbl_18, 'tbl_19': tbl_19, 'tbl_20': tbl_20, 'tbl_21': tbl_21, 'tbl_22': tbl_22, 'tbl_23': tbl_23, 'tbl_24': tbl_24, 'tbl_25': tbl_25, 'tbl_26': tbl_26, 'tbl_27': tbl_27, 'tbl_28': tbl_28, 'tbl_29': tbl_29, 'tbl_30': tbl_30, 'tbl_31': tbl_31, 'tbl_32': tbl_32, 'W_top1': W_top1, 'b_top1': b_top1, 'W_top2': W_top2, 'b_top2': b_top2, 'W_top3': W_top3, 'L0_rec_attn_W': _L0_rec_in['attn_W'], 'L0_rec_attn_b': _L0_rec_in['attn_b']}

def reference(r_gnn_feature, ids, tbl_0, tbl_1, tbl_2, tbl_3, tbl_4, tbl_5, tbl_6, tbl_7, tbl_8, tbl_9, tbl_10, tbl_11, tbl_12, tbl_13, tbl_14, tbl_15, tbl_16, tbl_17, tbl_18, tbl_19, tbl_20, tbl_21, tbl_22, tbl_23, tbl_24, tbl_25, tbl_26, tbl_27, tbl_28, tbl_29, tbl_30, tbl_31, tbl_32, W_top1, b_top1, W_top2, b_top2, W_top3, L0_rec_attn_W, L0_rec_attn_b):
    import jax
    import jax.numpy as jnp

    def _L0_rec_ref(gnn_feature, x, attn_W, attn_b):
        import jax, jax.numpy as jnp
        import numpy as np
        B, F, D, A = (1024, 33, 128, 128)
        num_fields = x.shape[1]
        row, col = np.triu_indices(num_fields, k=1)
        inner = x[:, row] * x[:, col]
        fm = jax.nn.relu(jnp.einsum('bpd,ad->bpa', inner, attn_W) + attn_b)
        scores = jnp.einsum('ba,bpa->bp', gnn_feature, fm)
        attn = jax.nn.softmax(scores, axis=1)
        attn_output = jnp.einsum('bp,bpd->bd', attn, inner) * 100.0
        return jnp.concatenate([gnn_feature, attn_output], axis=1)
    e = jnp.stack([tbl_0[ids[:, 0]], tbl_1[ids[:, 1]], tbl_2[ids[:, 2]], tbl_3[ids[:, 3]], tbl_4[ids[:, 4]], tbl_5[ids[:, 5]], tbl_6[ids[:, 6]], tbl_7[ids[:, 7]], tbl_8[ids[:, 8]], tbl_9[ids[:, 9]], tbl_10[ids[:, 10]], tbl_11[ids[:, 11]], tbl_12[ids[:, 12]], tbl_13[ids[:, 13]], tbl_14[ids[:, 14]], tbl_15[ids[:, 15]], tbl_16[ids[:, 16]], tbl_17[ids[:, 17]], tbl_18[ids[:, 18]], tbl_19[ids[:, 19]], tbl_20[ids[:, 20]], tbl_21[ids[:, 21]], tbl_22[ids[:, 22]], tbl_23[ids[:, 23]], tbl_24[ids[:, 24]], tbl_25[ids[:, 25]], tbl_26[ids[:, 26]], tbl_27[ids[:, 27]], tbl_28[ids[:, 28]], tbl_29[ids[:, 29]], tbl_30[ids[:, 30]], tbl_31[ids[:, 31]], tbl_32[ids[:, 32]]], axis=1)
    z = _L0_rec_ref(r_gnn_feature, e, L0_rec_attn_W, L0_rec_attn_b)
    z = z.reshape(z.shape[0], -1)
    h = jnp.concatenate([z, r_gnn_feature], axis=1)
    h = jnp.maximum(h @ W_top1 + b_top1, 0.0)
    h = jnp.maximum(h @ W_top2 + b_top2, 0.0)
    y = h @ W_top3
    return y

_drawn_inputs = setup_inputs


def setup_inputs(seed=0):
    import zlib

    import numpy as np

    out = dict(_drawn_inputs(seed))
    spreads = {'b_top1': (0.0, 0.47), 'b_top2': (0.0, 0.1)}
    factors = {'tbl_0': 8.0,
     'tbl_1': 8.0,
     'tbl_2': 8.0,
     'tbl_3': 8.0,
     'tbl_4': 8.0,
     'tbl_5': 8.0,
     'tbl_6': 8.0,
     'tbl_7': 8.0,
     'tbl_8': 8.0,
     'tbl_9': 8.0,
     'tbl_10': 8.0,
     'tbl_11': 8.0,
     'tbl_12': 8.0,
     'tbl_13': 8.0,
     'tbl_14': 8.0,
     'tbl_15': 8.0,
     'tbl_16': 8.0,
     'tbl_17': 8.0,
     'tbl_18': 8.0,
     'tbl_19': 8.0,
     'tbl_20': 8.0,
     'tbl_21': 8.0,
     'tbl_22': 8.0,
     'tbl_23': 8.0,
     'tbl_24': 8.0,
     'tbl_25': 8.0,
     'tbl_26': 8.0,
     'tbl_27': 8.0,
     'tbl_28': 8.0,
     'tbl_29': 8.0,
     'tbl_30': 8.0,
     'tbl_31': 8.0,
     'tbl_32': 8.0,
     'L0_rec_attn_W': 8.0,
     'L0_rec_attn_b': 8.0}
    for name, (base, spread) in spreads.items():
        noise = np.random.default_rng([zlib.crc32(name.encode()), seed]).standard_normal(out[name].shape)
        drawn = base * np.exp(spread * noise) if base else spread * noise
        out[name] = jnp.asarray(drawn.astype(out[name].dtype))
    for name, factor in factors.items():
        out[name] = (out[name] * factor).astype(out[name].dtype)
    return out
```

```python
from contextlib import ExitStack

import concourse.bass as bass
from concourse import mybir

F32 = mybir.dt.float32
I32 = mybir.dt.int32
ALU = mybir.AluOpType
ACT = mybir.ActivationFunctionType
AX = mybir.AxisListType

P = 128
FIELDS = 33
HOPS = FIELDS // 2
WIDE = FIELDS + HOPS
PAIRS = FIELDS * HOPS
HALF = PAIRS // 2
BATCH = 512
TILES = BATCH // P
QUADS = 4
STEPS = P // QUADS
BAND = FIELDS * WIDE
GROUP = 3
GPB = 3
ROWS = GROUP * GPB
POOLS = P // ROWS
LEFT = P - POOLS * ROWS
POOL_N = POOLS + 1
CHUNK = 4
CHUNKS = FIELDS // CHUNK + 1
BANKF = 512
SCALE = 100.0

POOL_AT = 4
TRANS_AT = 20
MLP_AT = 29
LAG = 2

H1, H2 = 512, 256
K1, C1, C2 = 3, H1 // P, H2 // P


def flat(tensor_ap, offset, dims):
    return bass.AP(tensor=tensor_ap.tensor, offset=offset, ap=dims)


def build(nc, gnn, ids, tables, w_top1, b_top1, w_top2, b_top2, w_top3, attn_w, attn_b, out):
    fields_dram = nc.dram_tensor("fields_scratch", (BATCH * FIELDS, P), F32, kind="Internal").ap()
    band_dram = nc.dram_tensor("band_scratch", (P, BAND), F32, kind="Internal").ap()

    with ExitStack() as ctx:
        def sb(name, shape, dtype=F32):
            return ctx.enter_context(nc.sbuf_tensor(name, shape, dtype))

        def sem(name):
            return ctx.enter_context(nc.semaphore(name))

        idx = sb("idx", [P, TILES, FIELDS], I32)
        ring = sb("ring", [P, 2 * CHUNK, P])
        e_t = [sb(f"e_t{i}", [P, P, WIDE]) for i in range(2)]
        inner = sb("inner", [P, 2, QUADS, PAIRS])
        fm = sb("fm", [P, 2, QUADS, PAIRS])
        gnn_nat = sb("gnn_nat", [P, TILES, P])
        gnn_t = sb("gnn_t", [P, BATCH])
        attn_w_nat = sb("attn_w_nat", [P, P])
        attn_w_t = sb("attn_w_t", [P, P])
        ident = sb("ident", [P, P])
        gnn_diag = sb("gnn_diag", [P, STEPS, QUADS, 32])
        gnn_col = sb("gnn_col", [P, 2, QUADS, 32])
        neg_max = sb("neg_max", [P, 1])
        exp_sum = sb("exp_sum", [P, 1])
        inv_sum = sb("inv_sum", [P, 1])
        exps = sb("exps", [P, PAIRS])
        attn = sb("attn", [P, PAIRS])
        zeros = sb("zeros", [P, BAND])
        rows = sb("rows", [GROUP * FIELDS, 2, GPB, P])
        band = sb("band", [GROUP * FIELDS, 2, GPB, GROUP, WIDE])
        pooled = sb("pooled", [P, ROWS * WIDE])
        attn_out = sb("attn_out", [P, P])
        w1 = sb("w1", [P, K1, H1])
        w2 = sb("w2", [P, C1, H2])
        w3 = sb("w3", [P, C2])
        b1 = sb("b1", [P, C1])
        b2 = sb("b2", [P, C2])
        ab = sb("ab", [P, 1])
        h1 = sb("h1", [P, C1, P])
        h2 = sb("h2", [P, C2, P])
        y = sb("y", [1, BATCH])

        x_ps = ctx.enter_context(nc.psum_tensor("x_ps", [P, 4, BANKF], F32))
        s_ps = ctx.enter_context(nc.psum_tensor("s_ps", [P, 2, BANKF], F32))
        m_ps = ctx.enter_context(nc.psum_tensor("m_ps", [P, 2, BANKF], F32))

        ids_loaded = sem("ids_loaded")
        gnn_loaded = sem("gnn_loaded")
        weights_loaded = sem("weights_loaded")
        ident_zero = sem("ident_zero")
        ident_ready = sem("ident_ready")
        cleared = sem("cleared")
        bands_zeroed = sem("bands_zeroed")
        setup_turned = sem("setup_turned")
        setup_copied = sem("setup_copied")
        gathered = [sem(f"gathered{i}") for i in range(2)]
        stored = [sem(f"stored{i}") for i in range(2)]
        turned = sem("turned")
        turn_copied = sem("turn_copied")
        diag_ready = sem("diag_ready")
        inner_ready = sem("inner_ready")
        col_ready = sem("col_ready")
        x_ready = sem("x_ready")
        fm_ready = sem("fm_ready")
        scores_done = sem("scores_done")
        max_ready = sem("max_ready")
        exp_done = sem("exp_done")
        inv_ready = sem("inv_ready")
        attn_ready = sem("attn_ready")
        band_stored = sem("band_stored")
        pool_loaded = [sem(f"pool_loaded{i}") for i in range(2)]
        pool_done = sem("pool_done")
        pool_read = sem("pool_read")
        pool_summed = sem("pool_summed")
        mlp_done = sem("mlp_done")
        h1_ready = sem("h1_ready")
        h2_ready = sem("h2_ready")
        y_ready = sem("y_ready")
        y_stored = sem("y_stored")

        gathered_per_tile = [16 * (FIELDS - CHUNK * (CHUNKS // 2)), 16 * CHUNK * (CHUNKS // 2)]
        stored_per_tile = [16 * (CHUNKS - CHUNKS // 2), 16 * (CHUNKS // 2)]
        pool_per_batch = 16 * (1 + GROUP)
        pool_per_tile = [pool_per_batch * (POOLS // 2) + 16 * (1 + LEFT), pool_per_batch * (POOLS // 2)]

        def gathered_by(t, c):
            if c == CHUNKS - 1:
                return gathered_per_tile[0] * (t + 1)
            return gathered_per_tile[c % 2] * t + 16 * CHUNK * (c // 2 + 1)

        block = ctx.enter_context(nc.Block())

        @block.sync
        def _(sp):
            sp.dma_start(idx[:, :, :], ids.rearrange("(t p) f -> p t f", p=P)).then_inc(ids_loaded, 16)
            sp.dma_start(attn_w_nat[:, :], attn_w).then_inc(gnn_loaded, 16)
            sp.dma_start(gnn_nat[:, :, :], gnn.rearrange("(t p) a -> p t a", p=P)).then_inc(gnn_loaded, 16)
            sp.wait_ge(cleared, 1)
            sp.dma_start(band_dram, zeros[:, :]).then_inc(bands_zeroed, 16)

            def store_chunk(t, c, half, width, count):
                sp.wait_ge(gathered[half], count)
                sp.dma_start(
                    flat(fields_dram, t * P * FIELDS * P + c * (CHUNK * P), [[FIELDS * P, P], [1, width * P]]),
                    ring[:, half * CHUNK:half * CHUNK + width, :].rearrange("p f d -> p (f d)"),
                ).then_inc(stored[half], 16)

            def store_tile(t):
                with sp.Fori(0, CHUNKS // 2) as i:
                    for half in range(2):
                        store_chunk(t, 2 * i + half, half, CHUNK,
                                    gathered_per_tile[half] * t + 16 * CHUNK + 16 * CHUNK * i)
                store_chunk(t, CHUNKS - 1, 0, 1, gathered_by(t, CHUNKS - 1))

            def load_pool(t, k, slot, free_at, row):
                if free_at is not None:
                    sp.wait_ge(pool_done, free_at)
                sp.dma_start(rows[:, slot, :, :],
                             flat(fields_dram, (t * P + row) * (FIELDS * P),
                                  [[P, GROUP * FIELDS], [GROUP * FIELDS * P, GPB], [1, P]])
                             ).then_inc(pool_loaded[slot], 16)
                for r in range(GROUP):
                    sp.dma_start(band[r * FIELDS:(r + 1) * FIELDS, slot, :, r, :],
                                 flat(band_dram, row * BAND + r * BAND,
                                      [[WIDE, FIELDS], [GROUP * BAND, GPB], [1, WIDE]])
                                 ).then_inc(pool_loaded[slot], 16)

            def pool_inputs(t):
                if t == 0:
                    sp.wait_ge(bands_zeroed, 16)
                    sp.wait_ge(cleared, 3)
                else:
                    for slot in range(2):
                        sp.wait_ge(pool_loaded[slot], pool_per_tile[slot] * t)
                sp.wait_ge(attn_ready, t + 1)
                sp.dma_start(flat(band_dram, 1, [[BAND, P], [WIDE + 1, FIELDS], [1, HOPS]]),
                             attn[:, :].rearrange("b (i k) -> b i k", k=HOPS)).then_inc(band_stored, 16)
                for half in range(2):
                    sp.wait_ge(stored[half], stored_per_tile[half] * (t + 1))
                sp.wait_ge(band_stored, 16 * (t + 1))
                for k in range(2):
                    load_pool(t, k, k, POOL_N * t if t else None, ROWS * k)
                with sp.Fori(1, POOLS // 2) as i:
                    for slot in range(2):
                        load_pool(t, 2 * i + slot, slot, 2 * i + (POOL_N * t + slot - 1),
                                  2 * ROWS * i + ROWS * slot)
                sp.wait_ge(pool_done, POOL_N * t + POOLS - 1)
                sp.dma_start(rows[0:LEFT * FIELDS, 0, 0, :],
                             flat(fields_dram, (t * P + POOLS * ROWS) * FIELDS * P, [[P, LEFT * FIELDS], [1, P]])
                             ).then_inc(pool_loaded[0], 16)
                for r in range(LEFT):
                    sp.dma_start(band[r * FIELDS:(r + 1) * FIELDS, 0, 0, r, :],
                                 flat(band_dram, (POOLS * ROWS + r) * BAND, [[WIDE, FIELDS], [1, WIDE]])
                                 ).then_inc(pool_loaded[0], 16)

            store_tile(0)
            for t in range(TILES):
                if t > 0:
                    pool_inputs(t - 1)
                if t + 1 < TILES:
                    store_tile(t + 1)
            pool_inputs(TILES - 1)
            sp.wait_ge(y_ready, TILES)
            sp.dma_start(out.rearrange("b o -> o b"), y[:, :]).then_inc(y_stored, 16)
            sp.wait_ge(y_stored, 16)

        @block.gpsimd
        def _(pool):
            pool.memset(ident[:, :], 0.0).then_inc(ident_zero, 1)
            pool.wait_ge(ident_zero, 1)
            pool.affine_select(out=ident[:, :], in_=ident[:, :], compare_op=ALU.not_equal, fill=1.0, base=0,
                               pattern=[[-1, P]], channel_multiplier=1).then_inc(ident_ready, 1)
            pool.wait_ge(ids_loaded, 16)
            for t in range(TILES):
                for c in range(CHUNKS):
                    half = c % 2
                    before = CHUNKS * t + (c - 2 if c >= 2 else c - 1 if c == 0 else c - 2)
                    if before >= 0:
                        pool.wait_ge(turned, before + 1)
                        pool.wait_ge(stored[half], stored_per_tile[half] * t + 16 * (c // 2))
                    for j in range(min(CHUNK, FIELDS - CHUNK * c)):
                        field = CHUNK * c + j
                        pool.indirect_dma_start(
                            ring[:, half * CHUNK + j, :], None, tables[field],
                            bass.IndirectOffsetOnAxis(ap=idx[:, t, field:field + 1], axis=0),
                        ).then_inc(gathered[half], 16)

        @block.tensor
        def _(pe):
            def pair_products(n, slot, first=False):
                pe.wait_ge(inner_ready, n + 1)
                for q in range(QUADS):
                    if not (first and q < 2):
                        pe.wait_ge(fm_ready, QUADS * n + (q - 1))
                    for h in range(2):
                        mm = pe.matmul(x_ps[:, 2 * (q % 2) + h, 0:HALF], attn_w_t[:, :],
                                       inner[:, slot, q, h * HALF:(h + 1) * HALF], start=True, stop=True)
                    mm.then_inc(x_ready, 1)

            def scores(n, slot, start=False, stop=False):
                pe.wait_ge(fm_ready, QUADS * n + QUADS)
                pe.wait_ge(col_ready, n + 1)
                for h in range(2):
                    for q in range(QUADS):
                        mm = pe.matmul(s_ps[32 * q:32 * q + 32, h, 0:HALF], gnn_col[:, slot, q, :],
                                       fm[:, slot, q, h * HALF:(h + 1) * HALF], start=start, stop=stop)
                mm.then_inc(scores_done, 1)

            def turn_chunk(t, c, half, width, count, copied):
                pe.wait_ge(gathered[half], count)
                if copied is not None:
                    pe.wait_ge(turn_copied, copied)
                for j in range(width):
                    mm = pe.transpose(m_ps[:, half, j * P:(j + 1) * P], ring[:, half * CHUNK + j, :], ident[:, :])
                mm.then_inc(turned, 1)

            def pool_batch(loaded, slot):
                pe.wait_ge(pool_loaded[slot], loaded)
                for g in range(GPB):
                    mm = pe.matmul(m_ps[:, slot, g * GROUP * WIDE:(g + 1) * GROUP * WIDE], rows[:, slot, g, :],
                                   band[:, slot, g, :, :].rearrange("p r w -> p (r w)"), start=True, stop=True)
                mm.then_inc(pool_done, 1)

            def pool_first(t, k):
                if k == 0:
                    pe.wait_ge(turn_copied, CHUNKS * min(t + 2, TILES))
                    if t > 0:
                        pe.wait_ge(h2_ready, C2 * t)
                else:
                    if t > 0:
                        pe.wait_ge(y_ready, t)
                pool_batch(pool_per_tile[k] * t + pool_per_batch, k)

            def pool_left(t):
                pe.wait_ge(pool_loaded[0], pool_per_tile[0] * (t + 1))
                pe.wait_ge(pool_read, POOL_N * t + POOLS - 1)
                pe.matmul(m_ps[:, 0, 0:LEFT * WIDE], rows[0:LEFT * FIELDS, 0, 0, :],
                          band[0:LEFT * FIELDS, 0, 0, 0:LEFT, :].rearrange("p r w -> p (r w)"),
                          start=True, stop=True).then_inc(pool_done, 1)

            def mlp_layer1(t):
                pe.wait_ge(pool_summed, POOL_N * (t + 1))
                if t + 2 < TILES:
                    pe.wait_ge(turn_copied, CHUNKS * (t + 3) - 1)
                g_cols = gnn_t[:, t * P:(t + 1) * P]
                for c in range(C1):
                    for n, (k, rhs) in enumerate(((0, g_cols), (2, g_cols), (1, attn_out[:, :]))):
                        mm = pe.matmul(m_ps[:, 1, c * P:(c + 1) * P], w1[:, k, c * P:(c + 1) * P], rhs,
                                       start=(n == 0), stop=(n == K1 - 1))
                mm.then_inc(mlp_done, 1)

            def mlp_layer2(t):
                pe.wait_ge(h1_ready, C1 * (t + 1))
                if t + 2 < TILES:
                    pe.wait_ge(turn_copied, CHUNKS * (t + 3))
                for c in range(C2):
                    for k in range(C1):
                        mm = pe.matmul(m_ps[:, 0, c * P:(c + 1) * P], w2[:, k, c * P:(c + 1) * P], h1[:, k, :],
                                       start=(k == 0), stop=(k == C1 - 1))
                mm.then_inc(mlp_done, 1)

            def mlp_layer3(t):
                pe.wait_ge(h2_ready, C2 * (t + 1))
                for k in range(C2):
                    mm = pe.matmul(m_ps[0:1, 1, 0:P], w3[:, k:k + 1], h2[:, k, :], start=(k == 0), stop=(k == C2 - 1))
                mm.then_inc(mlp_done, 1)

            pe.wait_ge(ident_ready, 1)
            pe.wait_ge(gnn_loaded, 32)
            pe.transpose(m_ps[:, 0, 0:P], attn_w_nat[:, :], ident[:, :]).then_inc(setup_turned, 1)
            for t in range(TILES):
                mm = pe.transpose(m_ps[:, 1, t * P:(t + 1) * P], gnn_nat[:, t, :], ident[:, :])
            mm.then_inc(setup_turned, 1)
            pe.wait_ge(setup_copied, 2)
            for c in range(CHUNKS):
                turn_chunk(0, c, c % 2, min(CHUNK, FIELDS - CHUNK * c), gathered_by(0, c), c - 1 if c >= 2 else None)

            for t in range(TILES):
                base = STEPS * t
                pair_products(base, 0, first=(t == 0))
                if t > 0:
                    scores(base - 1, 1, stop=True)
                pair_products(base + 1, 1)
                if t > 0:
                    pe.wait_ge(exp_done, t)
                scores(base, 0, start=True)
                for s in (2, 3):
                    pair_products(base + s, s % 2)
                    scores(base + s - 1, (s - 1) % 2)
                if t > 0:
                    for s in (POOL_AT, POOL_AT + 1):
                        pair_products(base + s, s % 2)
                        scores(base + s - 1, (s - 1) % 2)
                        pool_first(t - 1, s - POOL_AT)
                with pe.Fori(1 if t > 0 else 0, POOLS // 2) as i:
                    for j in range(2):
                        n = 2 * i + (base + POOL_AT + j)
                        pair_products(n, j)
                        scores(2 * i + (base + POOL_AT + j - 1), 1 - j)
                        if t > 0:
                            pe.wait_ge(pool_read, 2 * i + (POOL_N * (t - 1) + j - 1))
                            pool_batch(pool_per_batch * i + (pool_per_tile[j] * (t - 1) + pool_per_batch), j)
                for s in (18, 19):
                    pair_products(base + s, s % 2)
                    scores(base + s - 1, (s - 1) % 2)
                    if t > 0 and s == 18:
                        pool_left(t - 1)
                last = t + 1 == TILES
                if not last:
                    for s in (TRANS_AT, TRANS_AT + 1):
                        pair_products(base + s, s % 2)
                        scores(base + s - 1, (s - 1) % 2)
                        c = s - TRANS_AT
                        if t > 0:
                            pe.wait_ge(pool_read, POOL_N * t)
                        turn_chunk(t + 1, c, c, CHUNK, gathered_by(t + 1, c), CHUNKS * (t + 1))
                with pe.Fori(0 if last else 1, CHUNKS // 2) as i:
                    for j in range(2):
                        pair_products(2 * i + (base + TRANS_AT + j), j)
                        scores(2 * i + (base + TRANS_AT + j - 1), 1 - j)
                        if not last:
                            turn_chunk(t + 1, None, j, CHUNK,
                                       16 * CHUNK * i + (gathered_per_tile[j] * (t + 1) + 16 * CHUNK),
                                       2 * i + (CHUNKS * (t + 1) + j - 1))
                for s in range(28, STEPS):
                    pair_products(base + s, s % 2)
                    scores(base + s - 1, (s - 1) % 2)
                    if not last and s == 28:
                        turn_chunk(t + 1, CHUNKS - 1, 0, 1, gathered_by(t + 1, CHUNKS - 1), CHUNKS * (t + 1) + 7)
                    if t > 0 and s >= MLP_AT:
                        (mlp_layer1, mlp_layer2, mlp_layer3)[s - MLP_AT](t - 1)
            t = TILES - 1
            scores(STEPS * TILES - 1, 1, stop=True)
            pool_first(t, 0)
            pool_first(t, 1)
            with pe.Fori(1, POOLS // 2) as i:
                for j in range(2):
                    pe.wait_ge(pool_read, 2 * i + (POOL_N * t + j - 1))
                    pool_batch(pool_per_batch * i + (pool_per_tile[j] * t + pool_per_batch), j)
            pool_left(t)
            mlp_layer1(t)
            mlp_layer2(t)
            mlp_layer3(t)

        @block.scalar
        def _(act):
            act.dma_start(ab[:, :], attn_b.rearrange("(p o) -> p o", o=1)).then_inc(weights_loaded, 16)
            act.dma_start(w1[:, :, :], w_top1.rearrange("(k p) n -> p k n", p=P)).then_inc(weights_loaded, 16)
            act.dma_start(w2[:, :, :], w_top2.rearrange("(k p) n -> p k n", p=P)).then_inc(weights_loaded, 16)
            act.dma_start(w3[:, :], w_top3.rearrange("(k p) o -> p (k o)", p=P),
                          allow_slow_non_contiguous=True).then_inc(weights_loaded, 16)
            act.dma_start(b1[:, :], b_top1.rearrange("(c p) -> p c", p=P),
                          allow_slow_non_contiguous=True).then_inc(weights_loaded, 16)
            act.dma_start(b2[:, :], b_top2.rearrange("(c p) -> p c", p=P),
                          allow_slow_non_contiguous=True).then_inc(weights_loaded, 16)

            def relus(n, slot, first=False, behind_first_row=None):
                for q in range(QUADS):
                    act.wait_ge(x_ready, QUADS * n + (q + 1))
                    if q == 0 and not first:
                        act.wait_ge(scores_done, n - 1)
                    act.activation(fm[:, slot, q, :].rearrange("p (h n) -> p h n", h=2),
                                   x_ps[:, 2 * (q % 2):2 * (q % 2) + 2, 0:HALF],
                                   ACT.Relu, bias=ab[:, 0:1]).then_inc(fm_ready, 1)
                    if q == 0 and behind_first_row is not None:
                        exp_rows(behind_first_row)

            def exp_rows(t):
                act.wait_ge(max_ready, t + 1)
                if t > 0:
                    act.wait_ge(attn_ready, t)
                act.activation(exps[:, :].rearrange("p (h n) -> p h n", h=2), s_ps[:, :, 0:HALF], ACT.Exp,
                               bias=neg_max[:, 0:1], accum_out=exp_sum[:, 0:1]).then_inc(exp_done, 1)

            def mlp_relu(t, layer, width, bank, bias, h, ready):
                act.wait_ge(mlp_done, 3 * t + layer)
                for c in range(width):
                    act.activation(h[:, c, :], m_ps[:, bank, c * P:(c + 1) * P], ACT.Relu,
                                   bias=bias[:, c:c + 1]).then_inc(ready, 1)

            def mlp_out(t):
                act.wait_ge(mlp_done, 3 * t + 3)
                act.activation(y[0:1, t * P:(t + 1) * P], m_ps[0:1, 1, 0:P], ACT.Copy).then_inc(y_ready, 1)

            act.wait_ge(weights_loaded, 16 * 6)
            for t in range(TILES):
                base = STEPS * t
                relus(base, 0, first=(t == 0))
                relus(base + 1, 1, first=(t == 0), behind_first_row=t - 1 if t > 0 else None)
                with act.Fori(1, 14) as i:
                    for j in range(2):
                        relus(2 * i + (base + j), j)
                for s in range(28, STEPS):
                    relus(base + s, s % 2)
                    if t > 0 and s == MLP_AT:
                        mlp_relu(t - 1, 1, C1, 1, b1, h1, h1_ready)
                    if t > 0 and s == MLP_AT + 1:
                        mlp_relu(t - 1, 2, C2, 0, b2, h2, h2_ready)
                    if t > 0 and s == MLP_AT + 2:
                        mlp_out(t - 1)
            t = TILES - 1
            exp_rows(t)
            mlp_relu(t, 1, C1, 1, b1, h1, h1_ready)
            mlp_relu(t, 2, C2, 0, b2, h2, h2_ready)
            mlp_out(t)

        @block.vector
        def _(dve):
            def product(n, slot, t, m, first=False):
                if not first:
                    dve.wait_ge(x_ready, QUADS * n - QUADS)
                e = e_t[t % 2][:, :, :]
                dve.tensor_tensor(
                    inner[:, slot, :, :].rearrange("p q (i k) -> p q i k", k=HOPS),
                    flat(e, m * WIDE, [[P * WIDE, P], [32 * WIDE, QUADS], [1, FIELDS], [0, HOPS]]),
                    flat(e, m * WIDE + 1, [[P * WIDE, P], [32 * WIDE, QUADS], [1, FIELDS], [1, HOPS]]),
                    ALU.mult).then_inc(inner_ready, 1)

            def column(n, slot, m, first=False):
                if not first:
                    dve.wait_ge(scores_done, n - 1)
                dve.tensor_copy(gnn_col[:, slot, :, :],
                                flat(gnn_diag[:, :, :, :], m * (QUADS * 32), [[STEPS * QUADS * 32, P], [32, QUADS], [1, 32]])
                                ).then_inc(col_ready, 1)

            def copy_chunk(t, field, half, width, count, again):
                dve.wait_ge(turned, count)
                src = flat(m_ps[:, :, :], half * BANKF, [[2 * BANKF, P], [1, P], [P, width]])
                e = e_t[t % 2][:, :, :]
                cp = dve.tensor_copy(flat(e, field, [[P * WIDE, P], [WIDE, P], [1, width]]), src)
                if again:
                    cp = dve.tensor_copy(flat(e, field + FIELDS, [[P * WIDE, P], [WIDE, P], [1, width]]), src)
                cp.then_inc(turn_copied, 1)

            def pool_sum(t, count, slot, row, n_rows):
                dve.wait_ge(pool_done, count)
                dve.tensor_tensor(pooled[:, 0:n_rows * WIDE], m_ps[:, slot, 0:n_rows * WIDE],
                                  flat(e_t[t % 2][:, :, :], row * WIDE, [[P * WIDE, P], [1, n_rows * WIDE]]),
                                  ALU.mult).then_inc(pool_read, 1)
                dve.wait_ge(pool_read, count)
                dve.tensor_reduce(flat(attn_out[:, :], row, [[P, P], [1, n_rows]]),
                                  pooled[:, 0:n_rows * WIDE].rearrange("p (r w) -> p r w", w=WIDE),
                                  AX.X, ALU.add).then_inc(pool_summed, 1)
                dve.wait_ge(pool_summed, count)

            def row_max(t):
                dve.wait_ge(scores_done, STEPS * (t + 1))
                if t > 0:
                    dve.wait_ge(exp_done, t)
                dve.tensor_reduce(neg_max[:, 0:1], s_ps[:, :, 0:HALF], AX.XY, ALU.max,
                                  negate=True).then_inc(max_ready, 1)

            def normalise(t):
                dve.wait_ge(exp_done, t + 1)
                dve.reciprocal(inv_sum[:, :], exp_sum[:, :]).then_inc(inv_ready, 1)
                dve.wait_ge(inv_ready, t + 1)
                if t > 0:
                    dve.wait_ge(band_stored, 16 * t)
                dve.tensor_scalar(attn[:, :], exps[:, :], inv_sum[:, 0:1], SCALE, ALU.mult,
                                  ALU.mult).then_inc(attn_ready, 1)

            dve.memset(zeros[:, :], 0.0).then_inc(cleared, 1)
            dve.memset(gnn_diag[:, :, :, :], 0.0).then_inc(cleared, 1)
            dve.memset(band[:, :, :, :, :], 0.0).then_inc(cleared, 1)
            dve.wait_ge(setup_turned, 1)
            dve.tensor_copy(attn_w_t[:, :], m_ps[:, 0, 0:P]).then_inc(setup_copied, 1)
            dve.wait_ge(setup_turned, 2)
            dve.tensor_copy(gnn_t[:, :], m_ps[:, 1, :]).then_inc(setup_copied, 1)
            for c in range(CHUNKS):
                copy_chunk(0, CHUNK * c, c % 2, min(CHUNK, FIELDS - CHUNK * c), c + 1, c < HOPS // CHUNK)

            for t in range(TILES):
                base = STEPS * t
                if t == 0:
                    dve.wait_ge(setup_copied, 2)
                    dve.wait_ge(cleared, 2)
                else:
                    dve.wait_ge(col_ready, base)
                dve.tensor_copy(flat(gnn_diag[:, :, :, :], 0,
                                     [[STEPS * QUADS * 32, P], [32, QUADS], [QUADS * 32 + 1, STEPS]]),
                                gnn_t[:, t * P:(t + 1) * P].rearrange("a (q m) -> a q m", q=QUADS)
                                ).then_inc(diag_ready, 1)
                dve.wait_ge(turn_copied, CHUNKS * (t + 1))
                product(base, 0, t, 0, first=(t == 0))
                dve.wait_ge(diag_ready, t + 1)
                column(base, 0, 0, first=(t == 0))
                product(base + 1, 1, t, 1, first=(t == 0))
                column(base + 1, 1, 1, first=(t == 0))
                if t > 0:
                    row_max(t - 1)
                product(base + 2, 0, t, 2)
                column(base + 2, 0, 2)
                if t > 0:
                    normalise(t - 1)
                for s in (3, 4, 5):
                    product(base + s, s % 2, t, s)
                    column(base + s, s % 2, s)
                if t > 1:
                    dve.wait_ge(mlp_done, 3 * (t - 2) + 1)
                with dve.Fori(0, POOLS // 2) as i:
                    for j in range(2):
                        s0 = POOL_AT + LAG + j
                        product(2 * i + (base + s0), j, t, 2 * i + s0)
                        column(2 * i + (base + s0), j, 2 * i + s0)
                        if t > 0:
                            pool_sum(t - 1, 2 * i + (POOL_N * (t - 1) + j + 1), j, 2 * ROWS * i + ROWS * j, ROWS)
                for s in (20, 21):
                    product(base + s, s % 2, t, s)
                    column(base + s, s % 2, s)
                    if t > 0 and s == 20:
                        pool_sum(t - 1, POOL_N * t, 0, POOLS * ROWS, LEFT)
                for first_chunk, last_chunk in ((0, HOPS // CHUNK), (HOPS // CHUNK, CHUNKS - 1)):
                    with dve.Fori(first_chunk // 2, last_chunk // 2) as i:
                        for j in range(2):
                            s0 = TRANS_AT + LAG + j
                            product(2 * i + (base + s0), j, t, 2 * i + s0)
                            column(2 * i + (base + s0), j, 2 * i + s0)
                            if t + 1 < TILES:
                                copy_chunk(t + 1, 2 * CHUNK * i + CHUNK * j, j, CHUNK,
                                           2 * i + (CHUNKS * (t + 1) + j + 1), first_chunk == 0)
                for s in (30, 31):
                    product(base + s, s % 2, t, s)
                    column(base + s, s % 2, s)
                    if t + 1 < TILES and s == 30:
                        copy_chunk(t + 1, FIELDS - 1, 0, 1, CHUNKS * (t + 2), False)
            t = TILES - 1
            row_max(t)
            normalise(t)
            dve.wait_ge(mlp_done, 3 * (t - 1) + 1)
            with dve.Fori(0, POOLS // 2) as i:
                for j in range(2):
                    pool_sum(t, 2 * i + (POOL_N * t + j + 1), j, 2 * ROWS * i + ROWS * j, ROWS)
            pool_sum(t, POOL_N * (t + 1), 0, POOLS * ROWS, LEFT)


_INS = (["r_gnn_feature", "ids"] + [f"tbl_{f}" for f in range(FIELDS)]
        + ["W_top1", "b_top1", "W_top2", "b_top2", "W_top3", "L0_rec_attn_W", "L0_rec_attn_b"])


def kernel(**inputs):
    import numpy as np
    import concourse.bacc as bacc
    from concourse.bass_utils import run_bass_kernel_spmd

    nc = bacc.Bacc("TRN2", target_bir_lowering=False, num_devices=1)
    arrays, ap = {}, {}
    for name in _INS:
        a = np.ascontiguousarray(inputs[name])
        arrays[f"in_{name}"] = a
        ap[name] = nc.dram_tensor(f"in_{name}", a.shape, mybir.dt.from_np(a.dtype), kind="ExternalInput").ap()
    out = nc.dram_tensor("out_y", (BATCH, 1), F32, kind="ExternalOutput").ap()
    build(nc, ap["r_gnn_feature"], ap["ids"], [ap[f"tbl_{f}"] for f in range(FIELDS)], ap["W_top1"], ap["b_top1"],
          ap["W_top2"], ap["b_top2"], ap["W_top3"], ap["L0_rec_attn_W"], ap["L0_rec_attn_b"], out)
    result = run_bass_kernel_spmd(nc, [arrays], core_ids=[0])
    return result.results[0]["out_y"]
```

```python
from contextlib import ExitStack

import concourse.bass as bass
from concourse import mybir

F32 = mybir.dt.float32
I32 = mybir.dt.int32
ALU = mybir.AluOpType
ACT = mybir.ActivationFunctionType
AX = mybir.AxisListType

P = 128
FIELDS = 33
HOPS = FIELDS // 2
WIDE = FIELDS + HOPS
PAIRS = FIELDS * HOPS
HALF = PAIRS // 2
BATCH = 512
TILES = BATCH // P
QUADS = 4
STEPS = P // QUADS
BAND = FIELDS * WIDE
GROUP = 3
GPB = 3
ROWS = GROUP * GPB
POOLS = P // ROWS
LEFT = P - POOLS * ROWS
POOL_N = POOLS + 1
CHUNK = 4
CHUNKS = FIELDS // CHUNK + 1
BANKF = 512
SCALE = 100.0

POOL_AT = 4
TRANS_AT = 20
MLP1_AT, MLP2_AT = 29, 31
MLP3_AT = 1
LAST = TILES - 1
L_MLP1, L_MLP2, L_MLP3 = 21, 23, 24
L_POOL_AT = 25
STAGE_M = (0, 18, 28, STEPS)
L_BATCHES = (0, 8, 12)
TAIL_ROW = ROWS * L_BATCHES[2]
TAIL_GROUPS = (P - TAIL_ROW) // GROUP
LAG = 2

H1, H2 = 512, 256
K1, C1, C2 = 3, H1 // P, H2 // P


def flat(tensor_ap, offset, dims):
    return bass.AP(tensor=tensor_ap.tensor, offset=offset, ap=dims)


def build(nc, gnn, ids, tables, w_top1, b_top1, w_top2, b_top2, w_top3, attn_w, attn_b, out):
    fields_dram = nc.dram_tensor("fields_scratch", (BATCH * FIELDS, P), F32, kind="Internal").ap()
    band_dram = nc.dram_tensor("band_scratch", (P, BAND), F32, kind="Internal").ap()

    with ExitStack() as ctx:
        def sb(name, shape, dtype=F32):
            return ctx.enter_context(nc.sbuf_tensor(name, shape, dtype))

        def sem(name):
            return ctx.enter_context(nc.semaphore(name))

        idx = sb("idx", [P, TILES, FIELDS], I32)
        ring = sb("ring", [P, 2 * CHUNK, P])
        e_t = [sb(f"e_t{i}", [P, P, WIDE]) for i in range(2)]
        inner = sb("inner", [P, 2, QUADS, PAIRS])
        fm = sb("fm", [P, 2, QUADS, PAIRS])
        gnn_nat = sb("gnn_nat", [P, TILES, P])
        gnn_t = sb("gnn_t", [P, BATCH])
        attn_w_nat = sb("attn_w_nat", [P, P])
        attn_w_t = sb("attn_w_t", [P, P])
        ident = sb("ident", [P, P])
        gnn_diag = sb("gnn_diag", [P, STEPS, QUADS, 32])
        gnn_col = sb("gnn_col", [P, 2, QUADS, 32])
        neg_max = sb("neg_max", [P, 1])
        exp_sum = sb("exp_sum", [P, 1])
        inv_sum = sb("inv_sum", [P, 1])
        exps = sb("exps", [P, PAIRS])
        attn = sb("attn", [P, PAIRS])
        zeros = sb("zeros", [P, BAND])
        rows = sb("rows", [GROUP * FIELDS, 2, GPB, P])
        band = sb("band", [GROUP * FIELDS, 2, GPB, GROUP, WIDE])
        pooled = sb("pooled", [P, ROWS * WIDE])
        tail_rows = sb("tail_rows", [GROUP * FIELDS, TAIL_GROUPS + 1, P])
        tail_band = sb("tail_band", [GROUP * FIELDS, TAIL_GROUPS + 1, GROUP, WIDE])
        attn_out = sb("attn_out", [P, 2, P])
        w1 = sb("w1", [P, K1, H1])
        w2 = sb("w2", [P, C1, H2])
        w3 = sb("w3", [P, C2])
        b1 = sb("b1", [P, C1])
        b2 = sb("b2", [P, C2])
        ab = sb("ab", [P, 1])
        h1_gnn = sb("h1_gnn", [P, C1, BATCH])
        h1_sum = sb("h1_sum", [P, C1, P])
        h1 = sb("h1", [P, C1, P])
        h2 = sb("h2", [P, C2, P])
        y = sb("y", [1, BATCH])

        x_ps = ctx.enter_context(nc.psum_tensor("x_ps", [P, 4, BANKF], F32))
        s_ps = ctx.enter_context(nc.psum_tensor("s_ps", [P, 2, BANKF], F32))
        m_ps = ctx.enter_context(nc.psum_tensor("m_ps", [P, 2, BANKF], F32))

        ids_loaded = sem("ids_loaded")
        gnn_loaded = sem("gnn_loaded")
        biases_loaded = sem("biases_loaded")
        w1_loaded = sem("w1_loaded")
        w23_loaded = sem("w23_loaded")
        ident_zero = sem("ident_zero")
        ident_ready = sem("ident_ready")
        cleared = sem("cleared")
        bands_zeroed = sem("bands_zeroed")
        setup_turned = sem("setup_turned")
        setup_copied = sem("setup_copied")
        gathered = [sem(f"gathered{i}") for i in range(2)]
        stored = [sem(f"stored{i}") for i in range(2)]
        turned = sem("turned")
        turn_copied = sem("turn_copied")
        diag_ready = sem("diag_ready")
        inner_ready = sem("inner_ready")
        col_ready = sem("col_ready")
        x_ready = sem("x_ready")
        fm_ready = sem("fm_ready")
        scores_done = sem("scores_done")
        max_ready = sem("max_ready")
        exp_done = sem("exp_done")
        inv_ready = sem("inv_ready")
        attn_ready = sem("attn_ready")
        band_stored = sem("band_stored")
        pool_loaded = [sem(f"pool_loaded{i}") for i in range(2)]
        pool_done = sem("pool_done")
        pool_read = sem("pool_read")
        pool_summed = sem("pool_summed")
        mlp_done = sem("mlp_done")
        h1_ready = sem("h1_ready")
        h2_ready = sem("h2_ready")
        y_ready = sem("y_ready")
        gnn_layer_done = sem("gnn_layer_done")
        gnn_layer_read = sem("gnn_layer_read")
        h1_summed = sem("h1_summed")
        tail_rows_loaded = sem("tail_rows_loaded")
        tail_band_loaded = sem("tail_band_loaded")
        y_stored = sem("y_stored")

        gathered_per_tile = [16 * (FIELDS - CHUNK * (CHUNKS // 2)), 16 * CHUNK * (CHUNKS // 2)]
        stored_per_tile = [16 * (CHUNKS - CHUNKS // 2), 16 * (CHUNKS // 2)]
        pool_per_batch = 16 * (1 + GROUP)
        pool_per_tile = [pool_per_batch * (POOLS // 2) + 16 * (1 + LEFT), pool_per_batch * (POOLS // 2)]

        def gathered_by(t, c):
            if c == CHUNKS - 1:
                return gathered_per_tile[0] * (t + 1)
            return gathered_per_tile[c % 2] * t + 16 * CHUNK * (c // 2 + 1)

        block = ctx.enter_context(nc.Block())

        @block.sync
        def _(sp):
            sp.dma_start(idx[:, :, :], ids.rearrange("(t p) f -> p t f", p=P)).then_inc(ids_loaded, 16)
            sp.dma_start(attn_w_nat[:, :], attn_w).then_inc(gnn_loaded, 16)
            sp.dma_start(gnn_nat[:, :, :], gnn.rearrange("(t p) a -> p t a", p=P)).then_inc(gnn_loaded, 16)

            def store_chunk(t, c, half, width, count):
                sp.wait_ge(gathered[half], count)
                sp.dma_start(
                    flat(fields_dram, t * P * FIELDS * P + c * (CHUNK * P), [[FIELDS * P, P], [1, width * P]]),
                    ring[:, half * CHUNK:half * CHUNK + width, :].rearrange("p f d -> p (f d)"),
                ).then_inc(stored[half], 16)

            def store_tile(t):
                with sp.Fori(0, CHUNKS // 2) as i:
                    for half in range(2):
                        store_chunk(t, 2 * i + half, half, CHUNK,
                                    gathered_per_tile[half] * t + 16 * CHUNK + 16 * CHUNK * i)
                store_chunk(t, CHUNKS - 1, 0, 1, gathered_by(t, CHUNKS - 1))

            def store_bands(stage, m0, m1):
                sp.wait_ge(attn_ready, stage + 1)
                for q in range(QUADS):
                    sp.dma_start(flat(band_dram, (QUADS * m0 + q) * BAND + 1,
                                      [[QUADS * BAND, m1 - m0], [WIDE + 1, FIELDS], [1, HOPS]]),
                                 attn[32 * q + m0:32 * q + m1, :].rearrange("b (i k) -> b i k", k=HOPS)
                                 ).then_inc(band_stored, 16)
                sp.wait_ge(band_stored, 16 * QUADS * (stage + 1))

            def load_pool(t, slot, free_at, row):
                if free_at is not None:
                    sp.wait_ge(pool_done, free_at)
                sp.dma_start(rows[:, slot, :, :],
                             flat(fields_dram, (t * P + row) * (FIELDS * P),
                                  [[P, GROUP * FIELDS], [GROUP * FIELDS * P, GPB], [1, P]])
                             ).then_inc(pool_loaded[slot], 16)
                for r in range(GROUP):
                    sp.dma_start(band[r * FIELDS:(r + 1) * FIELDS, slot, :, r, :],
                                 flat(band_dram, row * BAND + r * BAND,
                                      [[WIDE, FIELDS], [GROUP * BAND, GPB], [1, WIDE]])
                                 ).then_inc(pool_loaded[slot], 16)

            def pool_inputs(t):
                for half in range(2):
                    sp.wait_ge(stored[half], stored_per_tile[half] * (t + 1))
                for k in range(2):
                    load_pool(t, k, POOL_N * t if t else None, ROWS * k)
                with sp.Fori(1, POOLS // 2) as i:
                    for slot in range(2):
                        load_pool(t, slot, 2 * i + (POOL_N * t + slot - 1), 2 * ROWS * i + ROWS * slot)
                sp.wait_ge(pool_done, POOL_N * t + POOLS - 1)
                sp.dma_start(rows[0:LEFT * FIELDS, 0, 0, :],
                             flat(fields_dram, (t * P + POOLS * ROWS) * FIELDS * P, [[P, LEFT * FIELDS], [1, P]])
                             ).then_inc(pool_loaded[0], 16)
                for r in range(LEFT):
                    sp.dma_start(band[r * FIELDS:(r + 1) * FIELDS, 0, 0, r, :],
                                 flat(band_dram, (POOLS * ROWS + r) * BAND, [[WIDE, FIELDS], [1, WIDE]])
                                 ).then_inc(pool_loaded[0], 16)
                for slot in range(2):
                    sp.wait_ge(pool_loaded[slot], pool_per_tile[slot] * (t + 1))

            store_tile(0)
            sp.wait_ge(cleared, 4)
            sp.dma_start(band_dram, zeros[:, :]).then_inc(bands_zeroed, 16)
            store_tile(1)
            sp.wait_ge(bands_zeroed, 16)
            for t in range(LAST):
                store_bands(t, 0, STEPS)
                pool_inputs(t)
                if t + 2 < TILES:
                    store_tile(t + 2)
            for half in range(2):
                sp.wait_ge(stored[half], stored_per_tile[half] * TILES)
            first = (LAST * P + TAIL_ROW) * FIELDS * P
            sp.dma_start(tail_rows[:, 0:TAIL_GROUPS, :],
                         flat(fields_dram, first, [[P, GROUP * FIELDS], [GROUP * FIELDS * P, TAIL_GROUPS], [1, P]])
                         ).then_inc(tail_rows_loaded, 16)
            sp.dma_start(tail_rows[0:LEFT * FIELDS, TAIL_GROUPS, :],
                         flat(fields_dram, first + TAIL_GROUPS * GROUP * FIELDS * P, [[P, LEFT * FIELDS], [1, P]])
                         ).then_inc(tail_rows_loaded, 16)
            for stage in range(2):
                store_bands(LAST + stage, STAGE_M[stage], STAGE_M[stage + 1])
                for k in range(L_BATCHES[stage], L_BATCHES[stage + 1]):
                    load_pool(LAST, k % 2, POOL_N * LAST + max(k - 1, 0), ROWS * k)
            store_bands(LAST + 2, STAGE_M[2], STAGE_M[3])
            for r in range(GROUP):
                groups = TAIL_GROUPS + (r < LEFT)
                sp.dma_start(tail_band[r * FIELDS:(r + 1) * FIELDS, 0:groups, r, :],
                             flat(band_dram, (TAIL_ROW + r) * BAND, [[WIDE, FIELDS], [GROUP * BAND, groups], [1, WIDE]])
                             ).then_inc(tail_band_loaded, 16)
            sp.wait_ge(y_ready, TILES)
            sp.dma_start(out.rearrange("b o -> o b"), y[:, :]).then_inc(y_stored, 16)
            sp.wait_ge(y_stored, 16)

        @block.gpsimd
        def _(pool):
            pool.memset(ident[:, :], 0.0).then_inc(ident_zero, 1)
            pool.wait_ge(ident_zero, 1)
            pool.affine_select(out=ident[:, :], in_=ident[:, :], compare_op=ALU.not_equal, fill=1.0, base=0,
                               pattern=[[-1, P]], channel_multiplier=1).then_inc(ident_ready, 1)
            pool.wait_ge(ids_loaded, 16)
            for t in range(TILES):
                for c in range(CHUNKS):
                    half = c % 2
                    before = CHUNKS * t + (c - 1 if c == 0 else c - 2)
                    if before >= 0:
                        pool.wait_ge(turned, before + 1)
                        pool.wait_ge(stored[half], stored_per_tile[half] * t + 16 * (c // 2))
                    for j in range(min(CHUNK, FIELDS - CHUNK * c)):
                        field = CHUNK * c + j
                        pool.indirect_dma_start(
                            ring[:, half * CHUNK + j, :], None, tables[field],
                            bass.IndirectOffsetOnAxis(ap=idx[:, t, field:field + 1], axis=0),
                        ).then_inc(gathered[half], 16)

        @block.tensor
        def _(pe):
            def pair_products(n, slot, first=False):
                for q in range(QUADS):
                    if first:
                        pe.wait_ge(inner_ready, q + 1)
                    elif q == 0:
                        pe.wait_ge(inner_ready, QUADS * n + QUADS)
                    for h in range(2):
                        if not (first and q < 2):
                            pe.wait_ge(fm_ready, 2 * QUADS * n + (2 * q + h - 3))
                        pe.matmul(x_ps[:, 2 * (q % 2) + h, 0:HALF], attn_w_t[:, :],
                                  inner[:, slot, q, h * HALF:(h + 1) * HALF], start=True, stop=True
                                  ).then_inc(x_ready, 1)

            def scores(n, slot, start=False, stop=False, reopened=False):
                pe.wait_ge(fm_ready, 2 * QUADS * n + 2 * QUADS)
                pe.wait_ge(col_ready, n + 1)
                for h in range(2):
                    for q in range(QUADS):
                        mm = pe.matmul(s_ps[32 * q:32 * q + 32, h, 0:HALF], gnn_col[:, slot, q, :],
                                       fm[:, slot, q, h * HALF:(h + 1) * HALF], start=start, stop=stop,
                                       skip_group_check=reopened)
                mm.then_inc(scores_done, 1)

            def turn_chunk(half, width, count, copied):
                pe.wait_ge(gathered[half], count)
                if copied is not None:
                    pe.wait_ge(turn_copied, copied)
                for j in range(width):
                    mm = pe.transpose(m_ps[:, half, j * P:(j + 1) * P], ring[:, half * CHUNK + j, :], ident[:, :])
                mm.then_inc(turned, 1)

            def pool_batch(loaded, slot, read):
                pe.wait_ge(pool_loaded[slot], loaded)
                if read is not None:
                    pe.wait_ge(pool_read, read)
                for g in range(GPB):
                    mm = pe.matmul(m_ps[:, slot, g * GROUP * WIDE:(g + 1) * GROUP * WIDE], rows[:, slot, g, :],
                                   band[:, slot, g, :, :].rearrange("p r w -> p (r w)"), start=True, stop=True)
                mm.then_inc(pool_done, 1)

            def pool_first(t, k):
                if t > 0:
                    if k == 0:
                        pe.wait_ge(y_ready, t)
                    else:
                        pe.wait_ge(h2_ready, C2 * t)
                pool_batch(pool_per_tile[k] * t + pool_per_batch, k, None)

            def pool_left(t):
                pe.wait_ge(pool_loaded[0], pool_per_tile[0] * (t + 1))
                pe.wait_ge(pool_read, POOL_N * t + POOLS - 1)
                pe.matmul(m_ps[:, 0, 0:LEFT * WIDE], rows[0:LEFT * FIELDS, 0, 0, :],
                          band[0:LEFT * FIELDS, 0, 0, 0:LEFT, :].rearrange("p r w -> p (r w)"),
                          start=True, stop=True).then_inc(pool_done, 1)

            def mlp_layer1(t):
                pe.wait_ge(pool_summed, POOL_N * (t + 1))
                if t + 2 < TILES:
                    pe.wait_ge(turn_copied, CHUNKS * (t + 3) - 1)
                for c in range(C1):
                    mm = pe.matmul(m_ps[:, 1, c * P:(c + 1) * P], w1[:, 1, c * P:(c + 1) * P],
                                   attn_out[:, t % 2, :], start=True, stop=True)
                mm.then_inc(mlp_done, 1)

            def mlp_layer2(t):
                pe.wait_ge(h1_ready, t + 1)
                for c in range(C2):
                    for k in range(C1):
                        mm = pe.matmul(m_ps[:, 1, c * P:(c + 1) * P], w2[:, k, c * P:(c + 1) * P], h1[:, k, :],
                                       start=(k == 0), stop=(k == C1 - 1))
                mm.then_inc(mlp_done, 1)

            def mlp_layer3(t):
                pe.wait_ge(h2_ready, C2 * (t + 1))
                for k in range(C2):
                    mm = pe.matmul(m_ps[0:1, 0, 0:P], w3[:, k:k + 1], h2[:, k, :], start=(k == 0), stop=(k == C2 - 1))
                mm.then_inc(mlp_done, 1)

            pe.wait_ge(ident_ready, 1)
            pe.wait_ge(gnn_loaded, 32)
            pe.transpose(m_ps[:, 0, 0:P], attn_w_nat[:, :], ident[:, :]).then_inc(setup_turned, 1)
            for t in range(TILES):
                mm = pe.transpose(m_ps[:, 1, t * P:(t + 1) * P], gnn_nat[:, t, :], ident[:, :])
            mm.then_inc(setup_turned, 1)
            pe.wait_ge(setup_copied, 2)
            for c in range(CHUNKS):
                turn_chunk(c % 2, min(CHUNK, FIELDS - CHUNK * c), gathered_by(0, c), c - 1 if c >= 2 else None)
                if c >= CHUNKS - 1 - C1 and c < CHUNKS - 1:
                    part = c - (CHUNKS - 1 - C1)
                    if part == 0:
                        pe.wait_ge(w1_loaded, 16)
                    for k in (0, 2):
                        mm = pe.matmul(x_ps[:, part, :], w1[:, k, part * P:(part + 1) * P], gnn_t[:, :],
                                       start=(k == 0), stop=(k == 2))
                    mm.then_inc(gnn_layer_done, 1)
            pe.wait_ge(gnn_layer_read, C1)
            pe.wait_ge(w23_loaded, 32)

            for t in range(TILES):
                base = STEPS * t
                pair_products(base, 0, first=(t == 0))
                if t > 0:
                    scores(base - 1, 1, stop=True)
                pair_products(base + 1, 1)
                if t > 0:
                    pe.wait_ge(exp_done, t)
                scores(base, 0, start=True)
                if t >= 2:
                    mlp_layer3(t - 2)
                for s in (2, 3):
                    pair_products(base + s, s % 2)
                    scores(base + s - 1, (s - 1) % 2)
                if t > 0:
                    for s in (POOL_AT, POOL_AT + 1):
                        pair_products(base + s, s % 2)
                        scores(base + s - 1, (s - 1) % 2)
                        pool_first(t - 1, s - POOL_AT)
                with pe.Fori(1 if t > 0 else 0, POOLS // 2) as i:
                    for j in range(2):
                        pair_products(2 * i + (base + POOL_AT + j), j)
                        scores(2 * i + (base + POOL_AT + j - 1), 1 - j)
                        if t > 0:
                            pool_batch(pool_per_batch * i + (pool_per_tile[j] * (t - 1) + pool_per_batch), j,
                                       2 * i + (POOL_N * (t - 1) + j - 1))
                if t == LAST:
                    break
                for s in (18, 19):
                    pair_products(base + s, s % 2)
                    scores(base + s - 1, (s - 1) % 2)
                    if t > 0 and s == 18:
                        pool_left(t - 1)
                for s in (TRANS_AT, TRANS_AT + 1):
                    pair_products(base + s, s % 2)
                    scores(base + s - 1, (s - 1) % 2)
                    c = s - TRANS_AT
                    if t > 0:
                        pe.wait_ge(pool_read, POOL_N * t)
                    turn_chunk(c, CHUNK, gathered_by(t + 1, c), CHUNKS * (t + 1))
                with pe.Fori(1, CHUNKS // 2) as i:
                    for j in range(2):
                        pair_products(2 * i + (base + TRANS_AT + j), j)
                        scores(2 * i + (base + TRANS_AT + j - 1), 1 - j)
                        turn_chunk(j, CHUNK, 16 * CHUNK * i + (gathered_per_tile[j] * (t + 1) + 16 * CHUNK),
                                   2 * i + (CHUNKS * (t + 1) + j - 1))
                for s in range(28, STEPS):
                    pair_products(base + s, s % 2)
                    scores(base + s - 1, (s - 1) % 2)
                    if s == 28:
                        turn_chunk(0, 1, gathered_by(t + 1, CHUNKS - 1), CHUNKS * (t + 1) + 7)
                    if t > 0 and s == MLP1_AT:
                        mlp_layer1(t - 1)
                    if t > 0 and s == MLP2_AT:
                        mlp_layer2(t - 1)

            base = STEPS * LAST

            def own_pool(k):
                if k < 2:
                    pool_first(LAST, k)
                else:
                    pool_batch(pool_per_tile[k % 2] * LAST + pool_per_batch * (k // 2 + 1), k % 2,
                               POOL_N * LAST + k - 1)

            for s in range(POOL_AT + POOLS, STEPS):
                pair_products(base + s, s % 2)
                if s - 1 in STAGE_M:
                    pe.wait_ge(exp_done, LAST + STAGE_M.index(s - 1))
                scores(base + s - 1, (s - 1) % 2, stop=s in STAGE_M, reopened=s - 1 >= STAGE_M[1])
                if s == POOL_AT + POOLS:
                    pool_left(LAST - 1)
                if s == L_MLP1:
                    mlp_layer1(LAST - 1)
                if s == L_MLP2:
                    mlp_layer2(LAST - 1)
                if s == L_MLP3:
                    mlp_layer3(LAST - 1)
                if s >= L_POOL_AT:
                    own_pool(s - L_POOL_AT)
            scores(STEPS * TILES - 1, 1, stop=True, reopened=True)
            for k in range(STEPS - L_POOL_AT, L_BATCHES[2]):
                own_pool(k)
            pe.wait_ge(tail_rows_loaded, 32)
            pe.wait_ge(tail_band_loaded, 16 * GROUP)
            for g in range(TAIL_GROUPS + 1):
                whole = g < TAIL_GROUPS
                n_rows = GROUP if whole else LEFT
                mm = pe.matmul(x_ps[:, g // GPB, (g % GPB) * GROUP * WIDE:((g % GPB) * GROUP + n_rows) * WIDE],
                               tail_rows[0:n_rows * FIELDS, g, :],
                               tail_band[0:n_rows * FIELDS, g, 0:n_rows, :].rearrange("p r w -> p (r w)"),
                               start=True, stop=True)
                if g % GPB == GPB - 1 or not whole:
                    mm.then_inc(pool_done, 1)
            mlp_layer1(LAST)
            mlp_layer2(LAST)
            mlp_layer3(LAST)

        @block.scalar
        def _(act):
            act.dma_start(ab[:, :], attn_b.rearrange("(p o) -> p o", o=1)).then_inc(biases_loaded, 16)
            act.dma_start(b1[:, :], b_top1.rearrange("(c p) -> p c", p=P),
                          allow_slow_non_contiguous=True).then_inc(biases_loaded, 16)
            act.dma_start(b2[:, :], b_top2.rearrange("(c p) -> p c", p=P),
                          allow_slow_non_contiguous=True).then_inc(biases_loaded, 16)
            act.wait_ge(turned, 2)
            act.dma_start(w1[:, :, :], w_top1.rearrange("(k p) n -> p k n", p=P)).then_inc(w1_loaded, 16)
            act.wait_ge(turned, 5)
            act.dma_start(w2[:, :, :], w_top2.rearrange("(k p) n -> p k n", p=P)).then_inc(w23_loaded, 16)
            act.dma_start(w3[:, :], w_top3.rearrange("(k p) o -> p (k o)", p=P),
                          allow_slow_non_contiguous=True).then_inc(w23_loaded, 16)

            def relus(n, slot, first=False, stage=None):
                for q in range(QUADS):
                    for h in range(2):
                        act.wait_ge(x_ready, 2 * QUADS * n + (2 * q + h + 1))
                        if q == 0 and h == 0 and not first:
                            act.wait_ge(scores_done, n - 1)
                        act.activation(fm[:, slot, q, h * HALF:(h + 1) * HALF], x_ps[:, 2 * (q % 2) + h, 0:HALF],
                                       ACT.Relu, bias=ab[:, 0:1]).then_inc(fm_ready, 1)
                    if q == 0 and stage is not None:
                        exp_rows(stage)

            def exp_rows(stage):
                act.wait_ge(max_ready, stage + 1)
                if stage > 0:
                    act.wait_ge(attn_ready, stage)
                act.activation(exps[:, :].rearrange("p (h n) -> p h n", h=2), s_ps[:, :, 0:HALF], ACT.Exp,
                               bias=neg_max[:, 0:1], accum_out=exp_sum[:, 0:1]).then_inc(exp_done, 1)

            def mlp_relu2(t):
                act.wait_ge(mlp_done, 3 * t + 2)
                for c in range(C2):
                    act.activation(h2[:, c, :], m_ps[:, 1, c * P:(c + 1) * P], ACT.Relu,
                                   bias=b2[:, c:c + 1]).then_inc(h2_ready, 1)

            def mlp_out(t):
                act.wait_ge(mlp_done, 3 * t + 3)
                act.activation(y[0:1, t * P:(t + 1) * P], m_ps[0:1, 0, 0:P], ACT.Copy).then_inc(y_ready, 1)

            act.wait_ge(biases_loaded, 48)
            for c in range(C1):
                act.wait_ge(gnn_layer_done, c + 1)
                act.activation(h1_gnn[:, c, :], x_ps[:, c, :], ACT.Identity,
                               bias=b1[:, c:c + 1]).then_inc(gnn_layer_read, 1)
            for t in range(TILES):
                base = STEPS * t
                relus(base, 0, first=(t == 0))
                relus(base + 1, 1, first=(t == 0), stage=t - 1 if t > 0 else None)
                if t >= 2:
                    mlp_out(t - 2)
                with act.Fori(1, 9 if t == LAST else 14) as i:
                    for j in range(2):
                        relus(2 * i + (base + j), j)
                for s in range(18 if t == LAST else 28, STEPS):
                    relus(base + s, s % 2,
                          stage=LAST + STAGE_M.index(s - 1) - 1 if t == LAST and s - 1 in STAGE_M else None)
                    if t > 0 and s == (L_MLP2 if t == LAST else MLP2_AT):
                        mlp_relu2(t - 1)
                    if t == LAST and s == L_MLP3:
                        mlp_out(t - 1)
            exp_rows(LAST + 2)
            mlp_relu2(LAST)
            mlp_out(LAST)

        @block.vector
        def _(dve):
            def product(n, slot, t, m, first=False):
                if not first:
                    dve.wait_ge(x_ready, 2 * QUADS * n - 2 * QUADS)
                e = e_t[t % 2][:, :, :]
                dve.tensor_tensor(
                    inner[:, slot, :, :].rearrange("p q (i k) -> p q i k", k=HOPS),
                    flat(e, m * (QUADS * WIDE), [[P * WIDE, P], [WIDE, QUADS], [1, FIELDS], [0, HOPS]]),
                    flat(e, m * (QUADS * WIDE) + 1, [[P * WIDE, P], [WIDE, QUADS], [1, FIELDS], [1, HOPS]]),
                    ALU.mult).then_inc(inner_ready, QUADS)

            def column(n, slot, m, first=False):
                if not first:
                    dve.wait_ge(scores_done, n - 1)
                dve.tensor_copy(gnn_col[:, slot, :, :],
                                flat(gnn_diag[:, :, :, :], m * (QUADS * 32), [[STEPS * QUADS * 32, P], [32, QUADS], [1, 32]])
                                ).then_inc(col_ready, 1)

            def copy_chunk(t, field, half, width, count, again):
                dve.wait_ge(turned, count)
                src = flat(m_ps[:, :, :], half * BANKF, [[2 * BANKF, P], [1, P], [P, width]])
                e = e_t[t % 2][:, :, :]
                cp = dve.tensor_copy(flat(e, field, [[P * WIDE, P], [WIDE, P], [1, width]]), src)
                if again:
                    cp = dve.tensor_copy(flat(e, field + FIELDS, [[P * WIDE, P], [WIDE, P], [1, width]]), src)
                cp.then_inc(turn_copied, 1)

            def pool_sum(t, count, bank, row, n_rows):
                dve.wait_ge(pool_done, count)
                dve.tensor_tensor(pooled[:, 0:n_rows * WIDE], bank[:, 0:n_rows * WIDE],
                                  flat(e_t[t % 2][:, :, :], row * WIDE, [[P * WIDE, P], [1, n_rows * WIDE]]),
                                  ALU.mult).then_inc(pool_read, 1)
                dve.wait_ge(pool_read, count)
                dve.tensor_reduce(flat(attn_out[:, :, :], (t % 2) * P + row, [[2 * P, P], [1, n_rows]]),
                                  pooled[:, 0:n_rows * WIDE].rearrange("p (r w) -> p r w", w=WIDE),
                                  AX.X, ALU.add).then_inc(pool_summed, 1)
                dve.wait_ge(pool_summed, count)

            def own_pool_sum(k):
                pool_sum(LAST, POOL_N * LAST + k + 1, m_ps[:, k % 2, :], ROWS * k, ROWS)

            def row_max(stage, steps):
                dve.wait_ge(scores_done, steps)
                if stage > 0:
                    dve.wait_ge(exp_done, stage)
                dve.tensor_reduce(neg_max[:, 0:1], s_ps[:, :, 0:HALF], AX.XY, ALU.max,
                                  negate=True).then_inc(max_ready, 1)

            def normalise(stage):
                dve.wait_ge(exp_done, stage + 1)
                dve.reciprocal(inv_sum[:, :], exp_sum[:, :]).then_inc(inv_ready, 1)
                dve.wait_ge(inv_ready, stage + 1)
                if stage > 0:
                    dve.wait_ge(band_stored, 16 * QUADS * stage)
                dve.tensor_scalar(attn[:, :], exps[:, :], inv_sum[:, 0:1], SCALE, ALU.mult,
                                  ALU.mult).then_inc(attn_ready, 1)

            def mlp_relu1(t):
                dve.wait_ge(mlp_done, 3 * t + 1)
                dve.tensor_tensor(h1_sum[:, :, :], m_ps[:, 1, :].rearrange("p (c b) -> p c b", c=C1),
                                  h1_gnn[:, :, t * P:(t + 1) * P], ALU.add).then_inc(h1_summed, 1)
                dve.wait_ge(h1_summed, t + 1)
                dve.tensor_scalar(h1[:, :, :], h1_sum[:, :, :], 0.0, None, ALU.max).then_inc(h1_ready, 1)

            dve.wait_ge(setup_turned, 1)
            dve.tensor_copy(attn_w_t[:, :], m_ps[:, 0, 0:P]).then_inc(setup_copied, 1)
            dve.wait_ge(setup_turned, 2)
            dve.tensor_copy(gnn_t[:, :], m_ps[:, 1, :]).then_inc(setup_copied, 1)
            dve.memset(gnn_diag[:, :, :, :], 0.0).then_inc(cleared, 1)
            dve.memset(band[:, :, :, :, :], 0.0).then_inc(cleared, 1)
            dve.memset(tail_band[:, :, :, :], 0.0).then_inc(cleared, 1)
            dve.memset(zeros[:, :], 0.0).then_inc(cleared, 1)
            for c in range(CHUNKS):
                copy_chunk(0, CHUNK * c, c % 2, min(CHUNK, FIELDS - CHUNK * c), c + 1, c < HOPS // CHUNK)
            dve.wait_ge(gnn_layer_read, C1)

            for t in range(TILES):
                base = STEPS * t
                dve.wait_ge(turn_copied, CHUNKS * (t + 1))
                if t == 0:
                    e = e_t[0][:, :, :]
                    for q in range(QUADS):
                        dve.tensor_tensor(
                            inner[:, 0, q, :].rearrange("p (i k) -> p i k", k=HOPS),
                            flat(e, q * WIDE, [[P * WIDE, P], [1, FIELDS], [0, HOPS]]),
                            flat(e, q * WIDE + 1, [[P * WIDE, P], [1, FIELDS], [1, HOPS]]),
                            ALU.mult).then_inc(inner_ready, 1)
                    dve.wait_ge(setup_copied, 2)
                    dve.wait_ge(cleared, 1)
                else:
                    product(base, 0, t, 0)
                    dve.wait_ge(col_ready, base)
                dve.tensor_copy(flat(gnn_diag[:, :, :, :], 0,
                                     [[STEPS * QUADS * 32, P], [32, QUADS], [QUADS * 32 + 1, STEPS]]),
                                gnn_t[:, t * P:(t + 1) * P].rearrange("a (m q) -> a q m", q=QUADS)
                                ).then_inc(diag_ready, 1)
                dve.wait_ge(diag_ready, t + 1)
                column(base, 0, 0, first=(t == 0))
                product(base + 1, 1, t, 1, first=(t == 0))
                column(base + 1, 1, 1, first=(t == 0))
                if t > 0:
                    row_max(t - 1, STEPS * t)
                product(base + 2, 0, t, 2)
                column(base + 2, 0, 2)
                if t > 0:
                    normalise(t - 1)
                for s in (3, 4, 5):
                    product(base + s, s % 2, t, s)
                    column(base + s, s % 2, s)
                if t > 2:
                    dve.wait_ge(mlp_done, 3 * (t - 3) + 1)
                with dve.Fori(0, POOLS // 2) as i:
                    for j in range(2):
                        s0 = POOL_AT + LAG + j
                        product(2 * i + (base + s0), j, t, 2 * i + s0)
                        column(2 * i + (base + s0), j, 2 * i + s0)
                        if t > 0:
                            pool_sum(t - 1, 2 * i + (POOL_N * (t - 1) + j + 1), m_ps[:, j, :],
                                     2 * ROWS * i + ROWS * j, ROWS)
                if t == LAST:
                    break
                for s in (20, 21):
                    product(base + s, s % 2, t, s)
                    column(base + s, s % 2, s)
                    if t > 0 and s == 20:
                        pool_sum(t - 1, POOL_N * t, m_ps[:, 0, :], POOLS * ROWS, LEFT)
                for first_chunk, last_chunk in ((0, HOPS // CHUNK), (HOPS // CHUNK, CHUNKS - 1)):
                    with dve.Fori(first_chunk // 2, last_chunk // 2) as i:
                        for j in range(2):
                            s0 = TRANS_AT + LAG + j
                            product(2 * i + (base + s0), j, t, 2 * i + s0)
                            column(2 * i + (base + s0), j, 2 * i + s0)
                            copy_chunk(t + 1, 2 * CHUNK * i + CHUNK * j, j, CHUNK,
                                       2 * i + (CHUNKS * (t + 1) + j + 1), first_chunk == 0)
                for s in (30, 31):
                    product(base + s, s % 2, t, s)
                    column(base + s, s % 2, s)
                    if s == 30:
                        copy_chunk(t + 1, FIELDS - 1, 0, 1, CHUNKS * (t + 2), False)
                    if t > 0 and s == MLP1_AT + LAG:
                        mlp_relu1(t - 1)

            base = STEPS * LAST
            for s in range(20, STEPS):
                if s - LAG in STAGE_M:
                    row_max(LAST + STAGE_M.index(s - LAG) - 1, base + s - LAG)
                product(base + s, s % 2, LAST, s)
                column(base + s, s % 2, s)
                if s - LAG in STAGE_M:
                    normalise(LAST + STAGE_M.index(s - LAG) - 1)
                if s == 20:
                    pool_sum(LAST - 1, POOL_N * LAST, m_ps[:, 0, :], POOLS * ROWS, LEFT)
                if s == L_MLP1 + LAG:
                    mlp_relu1(LAST - 1)
                    dve.wait_ge(mlp_done, 3 * (LAST - 2) + 1)
                if s >= L_POOL_AT + LAG:
                    own_pool_sum(s - LAG - L_POOL_AT)
            own_pool_sum(STEPS - LAG - L_POOL_AT)
            row_max(LAST + 2, STEPS * TILES)
            own_pool_sum(STEPS - LAG - L_POOL_AT + 1)
            normalise(LAST + 2)
            for k in range(STEPS - L_POOL_AT, L_BATCHES[2]):
                own_pool_sum(k)
            for k in range(L_BATCHES[2], POOL_N):
                pool_sum(LAST, POOL_N * LAST + k + 1, x_ps[:, k - L_BATCHES[2], :], ROWS * k,
                         ROWS if k < POOLS else LEFT)
            mlp_relu1(LAST)


_INS = (["r_gnn_feature", "ids"] + [f"tbl_{f}" for f in range(FIELDS)]
        + ["W_top1", "b_top1", "W_top2", "b_top2", "W_top3", "L0_rec_attn_W", "L0_rec_attn_b"])


def kernel(**inputs):
    import numpy as np
    import concourse.bacc as bacc
    from concourse.bass_utils import run_bass_kernel_spmd

    nc = bacc.Bacc("TRN2", target_bir_lowering=False, num_devices=1)
    arrays, ap = {}, {}
    for name in _INS:
        a = np.ascontiguousarray(inputs[name])
        arrays[f"in_{name}"] = a
        ap[name] = nc.dram_tensor(f"in_{name}", a.shape, mybir.dt.from_np(a.dtype), kind="ExternalInput").ap()
    out = nc.dram_tensor("out_y", (BATCH, 1), F32, kind="ExternalOutput").ap()
    build(nc, ap["r_gnn_feature"], ap["ids"], [ap[f"tbl_{f}"] for f in range(FIELDS)], ap["W_top1"], ap["b_top1"],
          ap["W_top2"], ap["b_top2"], ap["W_top3"], ap["L0_rec_attn_W"], ap["L0_rec_attn_b"], out)
    result = run_bass_kernel_spmd(nc, [arrays], core_ids=[0])
    return result.results[0]["out_y"]
```

```python
from contextlib import ExitStack

import concourse.bass as bass
from concourse import mybir

F32 = mybir.dt.float32
I32 = mybir.dt.int32
ALU = mybir.AluOpType
ACT = mybir.ActivationFunctionType
AX = mybir.AxisListType

P = 128
FIELDS = 33
HOPS = FIELDS // 2
WIDE = FIELDS + HOPS
PAIRS = FIELDS * HOPS
CUT = HOPS * HOPS
HALVES = ((0, CUT), (CUT, PAIRS))
BATCH = 512
TILES = BATCH // P
QUADS = 4
STEPS = P // QUADS
SIDE = FIELDS - 1
BAND = SIDE * WIDE
GROUP = P // SIDE
GPB = 3
ROWS = GROUP * GPB
POOLS = P // ROWS
LEFT_GROUPS = P // GROUP - POOLS * GPB
LEFT = LEFT_GROUPS * GROUP
POOL_N = POOLS + 1
CHUNK = 4
CHUNKS = FIELDS // CHUNK + 1
BANKF = 512
SCALE = 100.0

POOL_AT = 8
TRANS_AT = 20
LAST = TILES - 1
L_POOL_AT = 25
STAGE_M = (0, 18, 28, STEPS)
L_BATCHES = STAGE_M[1] * QUADS // ROWS
TAIL_ROW = ROWS * L_BATCHES
TAIL_GROUPS = (P - TAIL_ROW) // GROUP
TAIL_POOLS = -(-TAIL_GROUPS // GPB)
EARLY_GROUPS = (STAGE_M[2] * QUADS - TAIL_ROW) // GROUP
TAIL_BEFORE = 2
MLP_CUT = LAST * P + TAIL_ROW + TAIL_BEFORE * ROWS
MLP_PARTS = ((LAST * P - P, LAST * P, 0), (LAST * P, MLP_CUT, 0), (0, 2 * P, P), (MLP_CUT, BATCH, MLP_CUT - LAST * P))
T2, T3A, T01, T3B = range(len(MLP_PARTS))
LAG = 2

EARLY_STEPS = 6
BLOCK_I = CHUNK
BLOCKS = HOPS // BLOCK_I
BLOCK = BLOCK_I * HOPS
UNIT_STEPS = 2
UNIT = UNIT_STEPS * QUADS * BLOCK
UNITS = EARLY_STEPS // UNIT_STEPS
EARLY_UNITS = BLOCKS * UNITS

H1, H2 = 512, 256
K1, C1, C2 = 3, H1 // P, H2 // P


def flat(tensor_ap, offset, dims):
    return bass.AP(tensor=tensor_ap.tensor, offset=offset, ap=dims)


def build(nc, gnn, ids, tables, w_top1, b_top1, w_top2, b_top2, w_top3, attn_w, attn_b, out):
    fields_dram = nc.dram_tensor("fields_scratch", (BATCH * SIDE, P), F32, kind="Internal").ap()
    band_dram = nc.dram_tensor("band_scratch", (P, BAND), F32, kind="Internal").ap()

    with ExitStack() as ctx:
        def sb(name, shape, dtype=F32):
            return ctx.enter_context(nc.sbuf_tensor(name, shape, dtype))

        def sem(name):
            return ctx.enter_context(nc.semaphore(name))

        idx = sb("idx", [P, TILES, FIELDS], I32)
        ring = sb("ring", [P, 2 * CHUNK, P])
        e_t = [sb(f"e_t{i}", [P, P, WIDE]) for i in range(2)]
        inner = sb("inner", [P, 2, QUADS, PAIRS])
        fm = sb("fm", [P, 2, QUADS, PAIRS])
        gnn_nat = sb("gnn_nat", [P, TILES, P])
        gnn_t = sb("gnn_t", [P, BATCH])
        attn_w_nat = sb("attn_w_nat", [P, P])
        attn_w_t = sb("attn_w_t", [P, P])
        ident = sb("ident", [P, P])
        gnn_diag = sb("gnn_diag", [P, STEPS, QUADS, 32])
        gnn_col = sb("gnn_col", [P, 2, QUADS, 32])
        neg_max = sb("neg_max", [P, 1])
        exp_sum = sb("exp_sum", [P, 1])
        inv_sum = sb("inv_sum", [P, 1])
        exps = sb("exps", [P, PAIRS])
        attn = sb("attn", [P, PAIRS])
        zeros = sb("zeros", [P, BAND])
        rows = sb("rows", [P, 2, GPB, P])
        band = sb("band", [P, 2, GPB, GROUP, WIDE])
        pooled = sb("pooled", [P, ROWS * FIELDS])
        tail_rows = sb("tail_rows", [P, TAIL_GROUPS, P])
        tail_band = sb("tail_band", [P, TAIL_GROUPS, GROUP, WIDE])
        attn_out = sb("attn_out", [P, BATCH])
        w1 = sb("w1", [P, K1, H1])
        w2 = sb("w2", [P, C1, H2])
        w3 = sb("w3", [P, C2])
        b1 = sb("b1", [P, C1])
        b2 = sb("b2", [P, C2])
        ab = sb("ab", [P, 1])
        h1_gnn = sb("h1_gnn", [P, C1, BATCH])
        h1_sum = sb("h1_sum", [P, C1, 3 * P])
        h1 = sb("h1", [P, C1, 3 * P])
        h2 = sb("h2", [P, C2, 3 * P])
        y = sb("y", [1, BATCH])

        x_ps = ctx.enter_context(nc.psum_tensor("x_ps", [P, 4, BANKF], F32))
        s_ps = ctx.enter_context(nc.psum_tensor("s_ps", [P, 2, BANKF], F32))
        m_ps = ctx.enter_context(nc.psum_tensor("m_ps", [P, 2, BANKF], F32))

        ids_loaded = sem("ids_loaded")
        gnn_loaded = sem("gnn_loaded")
        biases_loaded = sem("biases_loaded")
        w1_loaded = sem("w1_loaded")
        w23_loaded = sem("w23_loaded")
        ident_zero = sem("ident_zero")
        ident_ready = sem("ident_ready")
        cleared = sem("cleared")
        bands_zeroed = sem("bands_zeroed")
        setup_turned = sem("setup_turned")
        setup_copied = sem("setup_copied")
        first_gathered = [sem(f"first_gathered{c}") for c in range(CHUNKS)]
        first_stored = sem("first_stored")
        gathered = [sem(f"gathered{i}") for i in range(2)]
        stored = [sem(f"stored{i}") for i in range(2)]
        turned = sem("turned")
        turn_copied = sem("turn_copied")
        diag_ready = sem("diag_ready")
        inner_ready = sem("inner_ready")
        col_ready = sem("col_ready")
        x_ready = sem("x_ready")
        fm_ready = sem("fm_ready")
        scores_done = sem("scores_done")
        max_ready = sem("max_ready")
        exp_done = sem("exp_done")
        inv_ready = sem("inv_ready")
        attn_ready = sem("attn_ready")
        band_stored = sem("band_stored")
        last_turned_stored = sem("last_turned_stored")
        pool_loaded = [sem(f"pool_loaded{i}") for i in range(2)]
        folded = sem("folded")
        tail_band_folded = sem("tail_band_folded")
        pool_done = sem("pool_done")
        pool_read = sem("pool_read")
        pool_summed = sem("pool_summed")
        layer1_done = sem("layer1_done")
        layer2_done = sem("layer2_done")
        layer3_done = sem("layer3_done")
        h1_ready = sem("h1_ready")
        h2_ready = sem("h2_ready")
        y_ready = sem("y_ready")
        early_inner = sem("early_inner")
        early_x = sem("early_x")
        early_fm = sem("early_fm")
        early_scored = sem("early_scored")
        gnn_layer_done = sem("gnn_layer_done")
        gnn_layer_read = sem("gnn_layer_read")
        h1_summed = sem("h1_summed")
        tail_rows_loaded = sem("tail_rows_loaded")
        tail_band_loaded = [sem(f"tail_band_loaded{i}") for i in range(2)]
        y_stored = sem("y_stored")

        first_fields = e_t[1][:, :, :].rearrange("p b i -> p (b i)")[:, 0:FIELDS * P].rearrange("p (f d) -> p f d", d=P)
        score_at = (BANKF - CUT, 0)
        all_scores = flat(s_ps[:, :, :], score_at[0], [[2 * BANKF, P], [1, PAIRS]])

        gathered_per_tile = [16 * (FIELDS - CHUNK * (CHUNKS // 2)), 16 * CHUNK * (CHUNKS // 2)]
        stored_per_tile = 16 * (SIDE // CHUNK // 2)
        pool_per_batch = 16 * (1 + GROUP)
        pool_per_tile = [pool_per_batch * (POOLS // 2 + 1), pool_per_batch * (POOLS // 2)]
        bands_per_stage = 16 * 2 * QUADS

        def early_at(tensor, u):
            return tensor[:, 0 if 4 <= u < 8 else 1, u % 4, 0:UNIT]

        def x_bank(q, h, late):
            return q if late else 2 * (q % 2) + h

        def gathered_by(t, c):
            if c == CHUNKS - 1:
                return gathered_per_tile[0] * t
            return gathered_per_tile[c % 2] * (t - 1) + 16 * CHUNK * (c // 2 + 1)

        def pools_through(part):
            if part == T3A:
                return POOL_N * LAST + L_BATCHES + TAIL_BEFORE
            if part == T3B:
                return POOL_N * LAST + L_BATCHES + TAIL_POOLS
            return POOL_N * (MLP_PARTS[part][1] // P)

        def chunk(bank, c, pitch, n):
            return bank[:, c * pitch:c * pitch + n]

        def layer1_psum(part, c):
            n = MLP_PARTS[part][1] - MLP_PARTS[part][0]
            if part == T01:
                return chunk(m_ps[:, c // 2, :], c % 2, 2 * P, n)
            return chunk(x_ps[:, 3, :] if part in (T2, T3A) else m_ps[:, 1, :], c, P, n)

        def layer2_psum(part, c):
            n = MLP_PARTS[part][1] - MLP_PARTS[part][0]
            return chunk(x_ps[:, 0, :], c, 2 * P, n) if part == T01 else chunk(s_ps[:, 0, :], c, P, n)

        def layer3_psum(part):
            n = MLP_PARTS[part][1] - MLP_PARTS[part][0]
            return (x_ps[:, 1, :] if part == T01 else s_ps[:, 1, :])[0:1, 0:n]

        def hidden(h, part):
            start, end, at = MLP_PARTS[part]
            return h[:, :, at:at + end - start]

        def issue_bands(queue, stage, m0, m1, main=range(QUADS), turned_around=range(QUADS), done=band_stored):
            queue.wait_ge(attn_ready, stage + 1)
            for q in main:
                queue.dma_start(flat(band_dram, (QUADS * m0 + q) * BAND + 1,
                                     [[QUADS * BAND, m1 - m0], [WIDE + 1, SIDE], [1, HOPS]]),
                                attn[32 * q + m0:32 * q + m1, 0:SIDE * HOPS].rearrange("b (i k) -> b i k", k=HOPS)
                                ).then_inc(done, 16)
            for q in turned_around:
                queue.dma_start(flat(band_dram, (QUADS * m0 + q) * BAND + SIDE,
                                     [[QUADS * BAND, m1 - m0], [WIDE, HOPS]]),
                                attn[32 * q + m0:32 * q + m1, SIDE * HOPS:PAIRS],
                                allow_slow_non_contiguous=True).then_inc(done, 16)

        def issue_tail_bands(queue, stage):
            if stage == 1:
                queue.wait_ge(band_stored, bands_per_stage * (LAST + 2))
            else:
                queue.wait_ge(band_stored, bands_per_stage * (LAST + 3) - 16 * 2)
                queue.wait_ge(last_turned_stored, 16 * 2)
            first, end = ((0, EARLY_GROUPS), (EARLY_GROUPS, TAIL_GROUPS))[stage - 1]
            for r in range(GROUP):
                queue.dma_start(tail_band[r * SIDE:(r + 1) * SIDE, first:end, r, :],
                                flat(band_dram, (TAIL_ROW + GROUP * first + r) * BAND,
                                     [[WIDE, SIDE], [GROUP * BAND, end - first], [1, WIDE]])
                                ).then_inc(tail_band_loaded[stage - 1], 16)

        tail_banks = [x_ps[:, i, :] for i in range(4)] + [m_ps[:, 0, :]]

        block = ctx.enter_context(nc.Block())

        @block.sync
        def _(sp):
            sp.dma_start(idx[:, :, :], ids.rearrange("(t p) f -> p t f", p=P)).then_inc(ids_loaded, 16)
            sp.dma_start(attn_w_nat[:, :], attn_w).then_inc(gnn_loaded, 16)
            sp.dma_start(gnn_nat[:, :, :], gnn.rearrange("(t p) a -> p t a", p=P)).then_inc(gnn_loaded, 16)

            for c in range(SIDE // CHUNK):
                sp.wait_ge(first_gathered[c], 16 * CHUNK)
                sp.dma_start(flat(fields_dram, c * (CHUNK * P), [[SIDE * P, P], [1, CHUNK * P]]),
                             first_fields[:, CHUNK * c:CHUNK * c + CHUNK, :].rearrange("p f d -> p (f d)")
                             ).then_inc(first_stored, 16)

            def store_chunk(t, c, half, count):
                sp.wait_ge(gathered[half], count)
                sp.dma_start(
                    flat(fields_dram, t * P * SIDE * P + c * (CHUNK * P), [[SIDE * P, P], [1, CHUNK * P]]),
                    ring[:, half * CHUNK:half * CHUNK + CHUNK, :].rearrange("p f d -> p (f d)"),
                ).then_inc(stored[half], 16)

            def store_tile(t):
                with sp.Fori(0, CHUNKS // 2) as i:
                    for half in range(2):
                        store_chunk(t, 2 * i + half, half,
                                    gathered_per_tile[half] * (t - 1) + 16 * CHUNK + 16 * CHUNK * i)

            def store_bands(stage, m0, m1):
                issue_bands(sp, stage, m0, m1)
                sp.wait_ge(band_stored, bands_per_stage * (stage + 1))

            def fields_stored(t):
                if t == 0:
                    sp.wait_ge(first_stored, 16 * (SIDE // CHUNK))
                else:
                    for half in range(2):
                        sp.wait_ge(stored[half], stored_per_tile * t)

            def load_pool(t, slot, free_at, row, groups=GPB):
                if free_at is not None:
                    sp.wait_ge(pool_done, free_at)
                sp.dma_start(rows[:, slot, 0:groups, :],
                             flat(fields_dram, (t * P + row) * (SIDE * P),
                                  [[P, P], [GROUP * SIDE * P, groups], [1, P]])
                             ).then_inc(pool_loaded[slot], 16)
                for r in range(GROUP):
                    sp.dma_start(band[r * SIDE:(r + 1) * SIDE, slot, 0:groups, r, :],
                                 flat(band_dram, row * BAND + r * BAND,
                                      [[WIDE, SIDE], [GROUP * BAND, groups], [1, WIDE]])
                                 ).then_inc(pool_loaded[slot], 16)

            def pool_inputs(t):
                fields_stored(t)
                for k in range(2):
                    load_pool(t, k, POOL_N * t if t else None, ROWS * k)
                with sp.Fori(1, POOLS // 2) as i:
                    for slot in range(2):
                        load_pool(t, slot, 2 * i + (POOL_N * t + slot - 1), 2 * ROWS * i + ROWS * slot)
                load_pool(t, 0, POOL_N * t + POOLS - 1, POOLS * ROWS, LEFT_GROUPS)
                for slot in range(2):
                    sp.wait_ge(pool_loaded[slot], pool_per_tile[slot] * (t + 1))

            sp.wait_ge(cleared, 4)
            sp.dma_start(band_dram, zeros[:, :]).then_inc(bands_zeroed, 16)
            store_tile(1)
            sp.wait_ge(bands_zeroed, 16)
            for t in range(LAST):
                store_bands(t, 0, STEPS)
                pool_inputs(t)
                if t + 2 < TILES:
                    store_tile(t + 2)
            fields_stored(LAST)
            sp.dma_start(tail_rows[:, :, :],
                         flat(fields_dram, (LAST * P + TAIL_ROW) * SIDE * P,
                              [[P, P], [GROUP * SIDE * P, TAIL_GROUPS], [1, P]])).then_inc(tail_rows_loaded, 16)
            store_bands(LAST, STAGE_M[0], STAGE_M[1])
            for k in range(L_BATCHES):
                load_pool(LAST, k % 2, POOL_N * LAST + max(k - 1, 0), ROWS * k)
            issue_bands(sp, LAST + 1, STAGE_M[1], STAGE_M[2])
            issue_tail_bands(sp, 1)
            issue_bands(sp, LAST + 2, STAGE_M[2], STAGE_M[3], turned_around=(0, 1))
            issue_tail_bands(sp, 2)
            sp.wait_ge(y_ready, len(MLP_PARTS))
            sp.dma_start(out.rearrange("b o -> o b"), y[:, :]).then_inc(y_stored, 16)
            sp.wait_ge(y_stored, 16)

        @block.gpsimd
        def _(pool):
            pool.memset(ident[:, :], 0.0).then_inc(ident_zero, 1)
            pool.wait_ge(ident_zero, 1)
            pool.affine_select(out=ident[:, :], in_=ident[:, :], compare_op=ALU.not_equal, fill=1.0, base=0,
                               pattern=[[-1, P]], channel_multiplier=1).then_inc(ident_ready, 1)
            pool.wait_ge(ids_loaded, 16)
            for c in range(CHUNKS):
                for field in range(CHUNK * c, min(CHUNK * c + CHUNK, FIELDS)):
                    pool.indirect_dma_start(
                        first_fields[:, field, :], None, tables[field],
                        bass.IndirectOffsetOnAxis(ap=idx[:, 0, field:field + 1], axis=0),
                    ).then_inc(first_gathered[c], 16)

            def gather_chunk(t, c):
                half = c % 2
                before = CHUNKS * t + (c - 1 if c == 0 else c - 2)
                if t > 1 or c >= 2:
                    pool.wait_ge(turned, before + 1)
                    pool.wait_ge(stored[half], stored_per_tile * (t - 1) + 16 * (c // 2))
                for j in range(min(CHUNK, FIELDS - CHUNK * c)):
                    field = CHUNK * c + j
                    pool.indirect_dma_start(
                        ring[:, half * CHUNK + j, :], None, tables[field],
                        bass.IndirectOffsetOnAxis(ap=idx[:, t, field:field + 1], axis=0),
                    ).then_inc(gathered[half], 16)

            def fold(view, done):
                pool.tensor_tensor(view[:, :, 0:HOPS], view[:, :, 0:HOPS], view[:, :, FIELDS:WIDE],
                                   ALU.add).then_inc(done, 1)

            def fold_batch(slot, loaded):
                pool.wait_ge(pool_loaded[slot], loaded)
                fold(band[:, slot, :, :, :].rearrange("p g r w -> p (g r) w"), folded)

            def fold_tile(t):
                with pool.Fori(0, POOLS // 2) as i:
                    for slot in range(2):
                        fold_batch(slot, pool_per_batch * i + (pool_per_tile[slot] * t + pool_per_batch))
                pool.wait_ge(pool_loaded[0], pool_per_tile[0] * (t + 1))
                fold(band[:, 0, 0:LEFT_GROUPS, :, :].rearrange("p g r w -> p (g r) w"), folded)

            for t in range(1, TILES):
                gather_chunk(t, 0)
                gather_chunk(t, 1)
                if t >= 2:
                    fold_tile(t - 2)
                for c in range(2, CHUNKS):
                    gather_chunk(t, c)
            fold_tile(LAST - 1)
            for k in range(L_BATCHES):
                fold_batch(k % 2, pool_per_tile[k % 2] * LAST + pool_per_batch * (k // 2 + 1))
            for stage in range(2):
                if stage == 1:
                    issue_bands(pool, LAST + 2, STAGE_M[2], STAGE_M[3], main=(), turned_around=(2, 3),
                                done=last_turned_stored)
                pool.wait_ge(tail_band_loaded[stage], 16 * GROUP)
                lo, hi = ((0, EARLY_GROUPS), (EARLY_GROUPS, TAIL_GROUPS))[stage]
                fold(tail_band[:, lo:hi, :, :].rearrange("p g r w -> p (g r) w"), tail_band_folded)

        @block.tensor
        def _(pe):
            def pair_products(n, slot, first=False, late=False):
                for q in range(QUADS):
                    if q == 0:
                        pe.wait_ge(inner_ready, QUADS * n + QUADS)
                    for h in range(1 if late else 0, 2):
                        if first:
                            pe.wait_ge(early_fm, EARLY_UNITS - 3 + q)
                        elif late:
                            pe.wait_ge(fm_ready, 2 * QUADS * (n - 1) + 2 * q + 2)
                        else:
                            pe.wait_ge(fm_ready, 2 * QUADS * n + (2 * q + h - 3))
                        lo, hi = HALVES[h]
                        pe.matmul(x_ps[:, x_bank(q, h, late), 0:hi - lo], attn_w_t[:, :],
                                  inner[:, slot, q, lo:hi], start=True, stop=True
                                  ).then_inc(x_ready, 2 if late else 1)

            def scores(n, slot, start=False, stop=False, reopened=False, late=False,
                       opened_early=False):
                pe.wait_ge(fm_ready, 2 * QUADS * n + 2 * QUADS)
                pe.wait_ge(col_ready, n + 1)
                for h in range(1 if late else 0, 2):
                    lo, hi = HALVES[h]
                    for q in range(QUADS):
                        mm = pe.matmul(s_ps[32 * q:32 * q + 32, h, score_at[h]:score_at[h] + hi - lo],
                                       gnn_col[:, slot, q, :], fm[:, slot, q, lo:hi],
                                       start=start, stop=stop, skip_group_check=reopened or (opened_early and h == 0))
                mm.then_inc(scores_done, 1)

            def turn_first(c):
                width = min(CHUNK, FIELDS - CHUNK * c)
                pe.wait_ge(first_gathered[c], 16 * width)
                if c >= 2:
                    pe.wait_ge(turn_copied, c - 1)
                for j in range(width):
                    mm = pe.transpose(m_ps[:, c % 2, j * P:(j + 1) * P], first_fields[:, CHUNK * c + j, :], ident[:, :])
                mm.then_inc(turned, 1)

            def open_early_scores():
                pe.wait_ge(cleared, 4)
                for q in range(QUADS):
                    pe.matmul(s_ps[32 * q:32 * q + 32, 0, score_at[0]:BANKF], zeros[:, 0:32], zeros[:, 0:CUT],
                              start=True, stop=True)

            def early_product(u):
                pe.wait_ge(early_inner, u + 1)
                if u < 4:
                    pe.wait_ge(gnn_layer_read, u + 1)
                else:
                    pe.wait_ge(early_fm, u - 3)
                pe.matmul(x_ps[:, u % 4, 0:UNIT], attn_w_t[:, :], early_at(inner, u),
                          start=True, stop=True).then_inc(early_x, 1)

            def early_scores(u):
                block, pair = u // UNITS, u % UNITS
                pe.wait_ge(early_fm, u + 1)
                at = score_at[0] + block * BLOCK
                for r in range(UNIT_STEPS):
                    for q in range(QUADS):
                        row = (r * QUADS + q) * BLOCK
                        mm = pe.matmul(s_ps[32 * q:32 * q + 32, 0, at:at + BLOCK],
                                       gnn_diag[:, UNIT_STEPS * pair + r, q, :], early_at(fm, u)[:, row:row + BLOCK],
                                       start=False, stop=True, skip_group_check=True)
                mm.then_inc(early_scored, 1)

            def turn_chunk(half, width, count, copied):
                pe.wait_ge(gathered[half], count)
                if copied is not None:
                    pe.wait_ge(turn_copied, copied)
                for j in range(width):
                    mm = pe.transpose(m_ps[:, half, j * P:(j + 1) * P], ring[:, half * CHUNK + j, :], ident[:, :])
                mm.then_inc(turned, 1)

            def pool_group(bank, g, fields, bands, done):
                sums = bank[:, g * GROUP * FIELDS:(g + 1) * GROUP * FIELDS]
                mm = pe.matmul(sums.rearrange("p (r w) -> p r w", w=FIELDS), fields, bands[:, :, 0:FIELDS], start=True, stop=True)
                if done:
                    mm.then_inc(pool_done, 1)

            def pool_batch(ready, slot, read, groups=GPB):
                pe.wait_ge(folded, ready)
                if read is not None:
                    pe.wait_ge(pool_read, read)
                for g in range(groups):
                    pool_group(m_ps[:, slot, :], g, rows[:, slot, g, :], band[:, slot, g, :, :], g == groups - 1)

            def pool_first(t, k):
                if t == LAST:
                    pe.wait_ge(pool_read, POOL_N * LAST)
                pool_batch(POOL_N * t + k + 1, k, None)

            def pool_left(t):
                pool_batch(POOL_N * (t + 1), 0, POOL_N * t + POOLS - 1, LEFT_GROUPS)

            def mlp_layer1(part):
                pe.wait_ge(pool_summed, pools_through(part))
                if part == T2:
                    pe.wait_ge(fm_ready, 2 * BATCH)
                if part == T01:
                    pe.wait_ge(pool_read, POOL_N * LAST + L_BATCHES)
                for c in range(C1):
                    mm = pe.matmul(layer1_psum(part, c), w1[:, 1, c * P:(c + 1) * P],
                                   attn_out[:, MLP_PARTS[part][0]:MLP_PARTS[part][1]], start=True, stop=True)
                mm.then_inc(layer1_done, 1)

            def mlp_layer2(part, chunks=range(C2)):
                pe.wait_ge(h1_ready, part + 1)
                if part == T2:
                    pe.wait_ge(exp_done, LAST + 3)
                for c in chunks:
                    for k in range(C1):
                        mm = pe.matmul(layer2_psum(part, c), w2[:, k, c * P:(c + 1) * P],
                                       hidden(h1, part)[:, k, :], start=(k == 0), stop=(k == C1 - 1))
                    mm.then_inc(layer2_done, 1)

            def mlp_layer3(part):
                pe.wait_ge(h2_ready, C2 * (part + 1))
                if part > T2:
                    pe.wait_ge(y_ready, part)
                for k in range(C2):
                    mm = pe.matmul(layer3_psum(part), w3[:, k:k + 1], hidden(h2, part)[:, k, :],
                                   start=(k == 0), stop=(k == C2 - 1))
                mm.then_inc(layer3_done, 1)

            pe.wait_ge(ident_ready, 1)
            pe.wait_ge(gnn_loaded, 32)
            pe.transpose(m_ps[:, 0, 0:P], attn_w_nat[:, :], ident[:, :]).then_inc(setup_turned, 1)
            for t in range(TILES):
                mm = pe.transpose(m_ps[:, 1, t * P:(t + 1) * P], gnn_nat[:, t, :], ident[:, :])
            mm.then_inc(setup_turned, 1)
            pe.wait_ge(setup_copied, 2)
            for c in range(BLOCKS + 1):
                turn_first(c)
                if c == 0:
                    pe.wait_ge(w1_loaded, 16)
                    continue
                for k in (0, 2):
                    mm = pe.matmul(x_ps[:, c - 1, :], w1[:, k, (c - 1) * P:c * P], gnn_t[:, :],
                                   start=(k == 0), stop=(k == 2))
                mm.then_inc(gnn_layer_done, 1)
                if c == BLOCKS - 1:
                    open_early_scores()
                    pe.wait_ge(diag_ready, 1)
            for u in range(EARLY_UNITS):
                early_product(u)
                if u > 0:
                    early_scores(u - 1)
                if u == 1 or (u >= UNITS and u % UNITS == 0):
                    turn_first(BLOCKS + 1 + u // UNITS)
            pe.wait_ge(w23_loaded, 32)

            for t in range(TILES):
                base = STEPS * t
                late = t == 0
                pair_products(base, 0, first=late, late=late)
                if t > 0:
                    scores(base - 1, 1, stop=True, opened_early=(t == 1))
                else:
                    early_scores(EARLY_UNITS - 1)
                pair_products(base + 1, 1, late=late)
                if t > 0:
                    pe.wait_ge(exp_done, t)
                scores(base, 0, start=True, late=late)
                for s in range(2, POOL_AT + 2):
                    late = t == 0 and s < EARLY_STEPS
                    late_before = t == 0 and s - 1 < EARLY_STEPS
                    pair_products(base + s, s % 2, late=late)
                    scores(base + s - 1, (s - 1) % 2, late=late_before, opened_early=t == 0 and not late_before)
                    if t > 0 and s >= POOL_AT:
                        pool_first(t - 1, s - POOL_AT)
                with pe.Fori(1, POOLS // 2) as i:
                    for j in range(2):
                        pair_products(2 * i + (base + POOL_AT + j), j)
                        scores(2 * i + (base + POOL_AT + j - 1), 1 - j, opened_early=(t == 0))
                        if t > 0:
                            pool_batch(2 * i + (POOL_N * (t - 1) + j + 1), j,
                                       2 * i + (POOL_N * (t - 1) + j - 1))
                if t == LAST:
                    break
                for s in (18, 19):
                    pair_products(base + s, s % 2)
                    scores(base + s - 1, (s - 1) % 2, opened_early=(t == 0))
                    if t > 0 and s == 18:
                        pool_left(t - 1)
                for s in (TRANS_AT, TRANS_AT + 1):
                    pair_products(base + s, s % 2)
                    scores(base + s - 1, (s - 1) % 2, opened_early=(t == 0))
                    c = s - TRANS_AT
                    if t > 0:
                        pe.wait_ge(pool_read, POOL_N * t)
                    turn_chunk(c, CHUNK, gathered_by(t + 1, c), CHUNKS * (t + 1))
                with pe.Fori(1, CHUNKS // 2) as i:
                    for j in range(2):
                        pair_products(2 * i + (base + TRANS_AT + j), j)
                        scores(2 * i + (base + TRANS_AT + j - 1), 1 - j, opened_early=(t == 0))
                        turn_chunk(j, CHUNK, 16 * CHUNK * i + (gathered_per_tile[j] * t + 16 * CHUNK),
                                   2 * i + (CHUNKS * (t + 1) + j - 1))
                for s in range(28, STEPS):
                    pair_products(base + s, s % 2)
                    scores(base + s - 1, (s - 1) % 2, opened_early=(t == 0))
                    if s == 28:
                        turn_chunk(0, 1, gathered_by(t + 1, CHUNKS - 1), CHUNKS * (t + 1) + 7)

            base = STEPS * LAST

            def own_pool(k):
                if k < 2:
                    pool_first(LAST, k)
                else:
                    pool_batch(POOL_N * LAST + k + 1, k % 2, POOL_N * LAST + k - 1)

            for s in range(POOL_AT + POOLS, STEPS):
                pair_products(base + s, s % 2)
                if s - 1 in STAGE_M:
                    pe.wait_ge(exp_done, LAST + STAGE_M.index(s - 1))
                scores(base + s - 1, (s - 1) % 2, stop=s in STAGE_M, reopened=s - 1 >= STAGE_M[1])
                if s == POOL_AT + POOLS:
                    pool_left(LAST - 1)
                if L_POOL_AT <= s < L_POOL_AT + L_BATCHES:
                    own_pool(s - L_POOL_AT)
            scores(STEPS * TILES - 1, 1, stop=True, reopened=True)
            mlp_layer1(T2)
            pe.wait_ge(tail_rows_loaded, 16)
            for g in range(TAIL_GROUPS):
                k = g // GPB
                if g == 0:
                    pe.wait_ge(tail_band_folded, 1)
                if g == TAIL_BEFORE * GPB:
                    mlp_layer2(T2)
                if k == 3 and g % GPB == 0:
                    mlp_layer3(T2)
                    mlp_layer1(T3A)
                    mlp_layer1(T01)
                    mlp_layer2(T3A)
                if g == EARLY_GROUPS:
                    mlp_layer2(T01, (0,))
                    pe.wait_ge(tail_band_folded, 2)
                if k == TAIL_POOLS - 1:
                    pe.wait_ge(pool_read, POOL_N * LAST + L_BATCHES - 1)
                pool_group(tail_banks[k], g % GPB, tail_rows[:, g, :], tail_band[:, g, :, :],
                           g % GPB == GPB - 1 or g == TAIL_GROUPS - 1)
            mlp_layer3(T3A)
            mlp_layer2(T01, (1,))
            mlp_layer1(T3B)
            mlp_layer3(T01)
            mlp_layer2(T3B)
            mlp_layer3(T3B)

        @block.scalar
        def _(act):
            act.dma_start(ab[:, :], attn_b.rearrange("(p o) -> p o", o=1)).then_inc(biases_loaded, 16)
            act.dma_start(b1[:, :], b_top1.rearrange("(c p) -> p c", p=P),
                          allow_slow_non_contiguous=True).then_inc(biases_loaded, 16)
            act.dma_start(b2[:, :], b_top2.rearrange("(c p) -> p c", p=P),
                          allow_slow_non_contiguous=True).then_inc(biases_loaded, 16)
            act.wait_ge(ids_loaded, 16)
            act.dma_start(w1[:, :, :], w_top1.rearrange("(k p) n -> p k n", p=P)).then_inc(w1_loaded, 16)

            def relus(n, slot, first=False, stage=None, late=False):
                for q in range(QUADS):
                    if q == 0 and first:
                        act.wait_ge(early_scored, (8, EARLY_UNITS)[slot])
                    elif q == 0:
                        act.wait_ge(scores_done, n - 1)
                    for h in range(1 if late else 0, 2):
                        act.wait_ge(x_ready, 2 * QUADS * n + (2 * q + h + 1))
                        lo, hi = HALVES[h]
                        act.activation(fm[:, slot, q, lo:hi], x_ps[:, x_bank(q, h, late), 0:hi - lo],
                                       ACT.Relu, bias=ab[:, 0:1]).then_inc(fm_ready, 2 if late else 1)
                    if q == 0 and stage is not None:
                        exp_rows(stage)

            def exp_rows(stage):
                act.wait_ge(max_ready, stage + 1)
                if stage > 0:
                    act.wait_ge(attn_ready, stage)
                act.activation(exps[:, :], all_scores, ACT.Exp,
                               bias=neg_max[:, 0:1], accum_out=exp_sum[:, 0:1]).then_inc(exp_done, 1)

            def mlp_relu2(part):
                act.wait_ge(layer2_done, C2 * part + C2)
                for c in range(C2):
                    act.activation(hidden(h2, part)[:, c, :], layer2_psum(part, c), ACT.Relu,
                                   bias=b2[:, c:c + 1]).then_inc(h2_ready, 1)

            def mlp_out(part):
                act.wait_ge(layer3_done, part + 1)
                act.activation(y[0:1, MLP_PARTS[part][0]:MLP_PARTS[part][1]], layer3_psum(part),
                               ACT.Copy).then_inc(y_ready, 1)

            act.wait_ge(biases_loaded, 48)
            for c in range(C1):
                act.wait_ge(gnn_layer_done, c + 1)
                act.activation(h1_gnn[:, c, :], x_ps[:, c, :], ACT.Identity,
                               bias=b1[:, c:c + 1]).then_inc(gnn_layer_read, 1)
            act.wait_ge(turned, C1 + 1)
            act.dma_start(w2[:, :, :], w_top2.rearrange("(k p) n -> p k n", p=P)).then_inc(w23_loaded, 16)
            act.dma_start(w3[:, :], w_top3.rearrange("(k p) o -> p (k o)", p=P),
                          allow_slow_non_contiguous=True).then_inc(w23_loaded, 16)
            for u in range(EARLY_UNITS):
                act.wait_ge(early_x, u + 1)
                if u >= 8:
                    act.wait_ge(early_scored, u - 7)
                act.activation(early_at(fm, u), x_ps[:, u % 4, 0:UNIT], ACT.Relu,
                               bias=ab[:, 0:1]).then_inc(early_fm, 1)
            for t in range(TILES):
                base = STEPS * t
                late = t == 0
                relus(base, 0, first=late, late=late)
                relus(base + 1, 1, first=late, late=late, stage=t - 1 if t > 0 else None)
                if t == 0:
                    for s in range(2, EARLY_STEPS):
                        relus(s, s % 2, late=True)
                with act.Fori(EARLY_STEPS // 2 if t == 0 else 1, 9 if t == LAST else 14) as i:
                    for j in range(2):
                        relus(2 * i + (base + j), j)
                for s in range(18 if t == LAST else 28, STEPS):
                    relus(base + s, s % 2,
                          stage=LAST + STAGE_M.index(s - 1) - 1 if t == LAST and s - 1 in STAGE_M else None)
            exp_rows(LAST + 2)
            for part in range(len(MLP_PARTS)):
                mlp_relu2(part)
                mlp_out(part)

        @block.vector
        def _(dve):
            def product(n, slot, t, m, late=False):
                if late and m < 2:
                    dve.wait_ge(early_x, (8, EARLY_UNITS)[m])
                else:
                    dve.wait_ge(x_ready, 2 * QUADS * n - 2 * QUADS)
                e = e_t[t % 2][:, :, :]
                i0 = HOPS if late else 0
                at = m * (QUADS * WIDE) + i0
                dve.tensor_tensor(
                    inner[:, slot, :, i0 * HOPS:PAIRS].rearrange("p q (i k) -> p q i k", k=HOPS),
                    flat(e, at, [[P * WIDE, P], [WIDE, QUADS], [1, FIELDS - i0], [0, HOPS]]),
                    flat(e, at + 1, [[P * WIDE, P], [WIDE, QUADS], [1, FIELDS - i0], [1, HOPS]]),
                    ALU.mult).then_inc(inner_ready, QUADS)

            def early_unit(u):
                block, pair = u // UNITS, u % UNITS
                if u >= 8:
                    dve.wait_ge(early_x, u - 7)
                e = e_t[0][:, :, :]
                n_rows = UNIT_STEPS * QUADS
                at = pair * n_rows * WIDE + block * BLOCK_I
                dve.tensor_tensor(
                    early_at(inner, u).rearrange("p (r i k) -> p r i k", i=BLOCK_I, k=HOPS),
                    flat(e, at, [[P * WIDE, P], [WIDE, n_rows], [1, BLOCK_I], [0, HOPS]]),
                    flat(e, at + 1, [[P * WIDE, P], [WIDE, n_rows], [1, BLOCK_I], [1, HOPS]]),
                    ALU.mult).then_inc(early_inner, 1)

            def diagonals(t):
                dve.tensor_copy(flat(gnn_diag[:, :, :, :], 0,
                                     [[STEPS * QUADS * 32, P], [32, QUADS], [QUADS * 32 + 1, STEPS]]),
                                gnn_t[:, t * P:(t + 1) * P].rearrange("a (m q) -> a q m", q=QUADS)
                                ).then_inc(diag_ready, 1)
                dve.wait_ge(diag_ready, t + 1)

            def column(n, slot, m, first=False):
                if not first:
                    dve.wait_ge(scores_done, n - 1)
                dve.tensor_copy(gnn_col[:, slot, :, :],
                                flat(gnn_diag[:, :, :, :], m * (QUADS * 32), [[STEPS * QUADS * 32, P], [32, QUADS], [1, 32]])
                                ).then_inc(col_ready, 1)

            def copy_chunk(t, field, half, width, count, again):
                dve.wait_ge(turned, count)
                src = flat(m_ps[:, :, :], half * BANKF, [[2 * BANKF, P], [1, P], [P, width]])
                e = e_t[t % 2][:, :, :]
                cp = dve.tensor_copy(flat(e, field, [[P * WIDE, P], [WIDE, P], [1, width]]), src)
                if again:
                    cp = dve.tensor_copy(flat(e, field + FIELDS, [[P * WIDE, P], [WIDE, P], [1, width]]), src)
                cp.then_inc(turn_copied, 1)

            def pool_sum(t, count, bank, row, n_rows):
                dve.wait_ge(pool_done, count)
                sums = pooled[:, 0:n_rows * FIELDS].rearrange("p (r w) -> p r w", w=FIELDS)
                dve.tensor_tensor(sums, bank[:, 0:n_rows * FIELDS].rearrange("p (r w) -> p r w", w=FIELDS),
                                  flat(e_t[t % 2][:, :, :], row * WIDE, [[P * WIDE, P], [WIDE, n_rows], [1, FIELDS]]),
                                  ALU.mult).then_inc(pool_read, 1)
                dve.wait_ge(pool_read, count)
                dve.tensor_reduce(flat(attn_out[:, :], t * P + row, [[BATCH, P], [1, n_rows]]),
                                  sums, AX.X, ALU.add).then_inc(pool_summed, 1)
                dve.wait_ge(pool_summed, count)

            def own_pool_sum(k):
                pool_sum(LAST, POOL_N * LAST + k + 1, m_ps[:, k % 2, :], ROWS * k, ROWS)

            def row_max(stage, steps):
                dve.wait_ge(scores_done, steps)
                if stage > 0:
                    dve.wait_ge(exp_done, stage)
                dve.tensor_reduce(neg_max[:, 0:1], all_scores, AX.X, ALU.max,
                                  negate=True).then_inc(max_ready, 1)

            def normalise(stage):
                dve.wait_ge(exp_done, stage + 1)
                dve.reciprocal(inv_sum[:, :], exp_sum[:, :]).then_inc(inv_ready, 1)
                dve.wait_ge(inv_ready, stage + 1)
                if stage > 0:
                    dve.wait_ge(band_stored, bands_per_stage * stage)
                dve.tensor_scalar(attn[:, :], exps[:, :], inv_sum[:, 0:1], SCALE, ALU.mult,
                                  ALU.mult).then_inc(attn_ready, 1)

            def mlp_relu1(part):
                start, end, _ = MLP_PARTS[part]
                if part == T01:
                    psum = m_ps[:, :, :].rearrange("p j n -> p (j n)").rearrange("p (c b) -> p c b", c=C1)
                else:
                    bank = m_ps[:, 1, :] if part == T3B else x_ps[:, 3, :]
                    psum = bank.rearrange("p (c b) -> p c b", c=C1)
                dve.wait_ge(layer1_done, part + 1)
                dve.tensor_tensor(hidden(h1_sum, part), psum[:, :, 0:end - start],
                                  h1_gnn[:, :, start:end], ALU.add).then_inc(h1_summed, 1)
                dve.wait_ge(h1_summed, part + 1)
                dve.tensor_scalar(hidden(h1, part), hidden(h1_sum, part), 0.0, None, ALU.max).then_inc(h1_ready, 1)

            dve.wait_ge(setup_turned, 1)
            dve.tensor_copy(attn_w_t[:, :], m_ps[:, 0, 0:P]).then_inc(setup_copied, 1)
            dve.wait_ge(setup_turned, 2)
            dve.tensor_copy(gnn_t[:, :], m_ps[:, 1, :]).then_inc(setup_copied, 1)
            dve.memset(gnn_diag[:, :, :, :], 0.0).then_inc(cleared, 1)
            dve.memset(band[:, :, :, :, :], 0.0).then_inc(cleared, 1)
            dve.memset(tail_band[:, :, :, :], 0.0).then_inc(cleared, 1)
            dve.memset(zeros[:, :], 0.0).then_inc(cleared, 1)
            dve.wait_ge(setup_copied, 2)
            dve.wait_ge(cleared, 1)
            diagonals(0)
            for c in range(CHUNKS):
                copy_chunk(0, CHUNK * c, c % 2, min(CHUNK, FIELDS - CHUNK * c), c + 1, c < HOPS // CHUNK)
                if BLOCKS <= c < 2 * BLOCKS:
                    dve.wait_ge(turn_copied, c + 1)
                    for pair in range(UNITS):
                        early_unit((c - BLOCKS) * UNITS + pair)
            dve.wait_ge(gnn_layer_read, C1)

            for t in range(TILES):
                base = STEPS * t
                dve.wait_ge(turn_copied, CHUNKS * (t + 1))
                late = t == 0
                product(base, 0, t, 0, late=late)
                if t > 0:
                    dve.wait_ge(col_ready, base)
                    diagonals(t)
                column(base, 0, 0, first=late)
                product(base + 1, 1, t, 1, late=late)
                column(base + 1, 1, 1, first=late)
                if t > 0:
                    row_max(t - 1, STEPS * t)
                product(base + 2, 0, t, 2, late=late)
                column(base + 2, 0, 2)
                if t > 0:
                    normalise(t - 1)
                for s in range(3, POOL_AT + LAG):
                    product(base + s, s % 2, t, s, late=t == 0 and s < EARLY_STEPS)
                    column(base + s, s % 2, s)
                with dve.Fori(0, POOLS // 2) as i:
                    for j in range(2):
                        s0 = POOL_AT + LAG + j
                        product(2 * i + (base + s0), j, t, 2 * i + s0)
                        column(2 * i + (base + s0), j, 2 * i + s0)
                        if t > 0:
                            pool_sum(t - 1, 2 * i + (POOL_N * (t - 1) + j + 1), m_ps[:, j, :],
                                     2 * ROWS * i + ROWS * j, ROWS)
                if t == LAST:
                    break
                for s in (20, 21):
                    product(base + s, s % 2, t, s)
                    column(base + s, s % 2, s)
                    if t > 0 and s == 20:
                        pool_sum(t - 1, POOL_N * t, m_ps[:, 0, :], POOLS * ROWS, LEFT)
                if t == 0:
                    dve.wait_ge(first_stored, 16 * (SIDE // CHUNK))
                for first_chunk, last_chunk in ((0, HOPS // CHUNK), (HOPS // CHUNK, CHUNKS - 1)):
                    with dve.Fori(first_chunk // 2, last_chunk // 2) as i:
                        for j in range(2):
                            s0 = TRANS_AT + LAG + j
                            product(2 * i + (base + s0), j, t, 2 * i + s0)
                            column(2 * i + (base + s0), j, 2 * i + s0)
                            copy_chunk(t + 1, 2 * CHUNK * i + CHUNK * j, j, CHUNK,
                                       2 * i + (CHUNKS * (t + 1) + j + 1), first_chunk == 0)
                for s in (30, 31):
                    product(base + s, s % 2, t, s)
                    column(base + s, s % 2, s)
                    if s == 30:
                        copy_chunk(t + 1, FIELDS - 1, 0, 1, CHUNKS * (t + 2), False)

            base = STEPS * LAST
            for s in range(20, STEPS):
                if s - LAG in STAGE_M:
                    row_max(LAST + STAGE_M.index(s - LAG) - 1, base + s - LAG)
                product(base + s, s % 2, LAST, s)
                column(base + s, s % 2, s)
                if s - LAG in STAGE_M:
                    normalise(LAST + STAGE_M.index(s - LAG) - 1)
                if s == 20:
                    pool_sum(LAST - 1, POOL_N * LAST, m_ps[:, 0, :], POOLS * ROWS, LEFT)
                if s >= L_POOL_AT + LAG:
                    own_pool_sum(s - LAG - L_POOL_AT)
            own_pool_sum(L_BATCHES - 1)
            row_max(LAST + 2, STEPS * TILES)
            mlp_relu1(T2)
            normalise(LAST + 2)
            for k in range(TAIL_POOLS):
                row = TAIL_ROW + k * ROWS
                pool_sum(LAST, POOL_N * LAST + L_BATCHES + k + 1, tail_banks[k], row, min(ROWS, P - row))
                if k == TAIL_BEFORE - 1:
                    mlp_relu1(T3A)
                    mlp_relu1(T01)
            mlp_relu1(T3B)


_INS = (["r_gnn_feature", "ids"] + [f"tbl_{f}" for f in range(FIELDS)]
        + ["W_top1", "b_top1", "W_top2", "b_top2", "W_top3", "L0_rec_attn_W", "L0_rec_attn_b"])


def kernel(**inputs):
    import numpy as np
    import concourse.bacc as bacc
    from concourse.bass_utils import run_bass_kernel_spmd

    nc = bacc.Bacc("TRN2", target_bir_lowering=False, num_devices=1)
    arrays, ap = {}, {}
    for name in _INS:
        a = np.ascontiguousarray(inputs[name])
        arrays[f"in_{name}"] = a
        ap[name] = nc.dram_tensor(f"in_{name}", a.shape, mybir.dt.from_np(a.dtype), kind="ExternalInput").ap()
    out = nc.dram_tensor("out_y", (BATCH, 1), F32, kind="ExternalOutput").ap()
    build(nc, ap["r_gnn_feature"], ap["ids"], [ap[f"tbl_{f}"] for f in range(FIELDS)], ap["W_top1"], ap["b_top1"],
          ap["W_top2"], ap["b_top2"], ap["W_top3"], ap["L0_rec_attn_W"], ap["L0_rec_attn_b"], out)
    result = run_bass_kernel_spmd(nc, [arrays], core_ids=[0])
    return result.results[0]["out_y"]
```
